# Optimizing a Trainium2 kernel written in Bass

```python
import numpy as np
import jax
import jax.numpy as jnp

def _softmax(x, axis=-1):
    return jax.nn.softmax(x, axis=axis)

def _gelu(x):
    return jax.nn.gelu(x, approximate=True)

def _silu(x):
    return jax.nn.silu(x)

def _sigmoid(x):
    return jax.nn.sigmoid(x)

def _layernorm(x, axis=-1, eps=1e-05):
    m = jnp.mean(x, axis=axis, keepdims=True)
    v = jnp.var(x, axis=axis, keepdims=True)
    return (x - m) / jnp.sqrt(v + eps)

def _scatter_add(tgt, idx, src, axis=0):
    return tgt.at[idx].add(src)

def _segment_sum(src, seg, n):
    return jax.ops.segment_sum(src, seg, n)
kernel_name = 'mk_gnn_resnorm_d2_gnn_r16_fe7fdb'

def setup_inputs(seed: int=0):
    np.random.seed(seed)
    _w = jnp.asarray

    def _rec_inputs():
        import jax
        import jax.numpy as jnp
        _gk = jax.random.key(seed)
        x = -0.0003713 + 1 * jax.random.normal(jax.random.fold_in(_gk, 1), (6250, 128), jnp.float32)
        src = jax.random.randint(jax.random.fold_in(_gk, 2), (200000,), 0, 6250, jnp.int32)
        dst = jax.random.randint(jax.random.fold_in(_gk, 3), (200000,), 0, 6250, jnp.int32)
        _o = jnp.argsort(dst, stable=True)
        src = src[_o]
        dst = dst[_o]
        edge_weight = jax.random.uniform(jax.random.fold_in(_gk, 12), (200000,), jnp.float32, 0.0, 0.999999)
        return (x, src, dst, edge_weight)
    x, src, dst, edge_weight = _rec_inputs()

    def _L0_gnn_setup():
        import jax, jax.numpy as jnp
        import numpy as np
        N = 6250
        E = 100000
        H = 128
        L = 3

        def _gru_cell(m, h, w_ih, w_hh, b_ih, b_hh):
            gi = m @ w_ih.T + b_ih
            gh = h @ w_hh.T + b_hh
            i_r, i_z, i_n = jnp.split(gi, 3, axis=-1)
            h_r, h_z, h_n = jnp.split(gh, 3, axis=-1)
            r = jax.nn.sigmoid(i_r + h_r)
            zg = jax.nn.sigmoid(i_z + h_z)
            n = jnp.tanh(i_n + r * h_n)
            return (1.0 - zg) * n + zg * h
        key = jax.random.key(seed)
        ks = jax.random.split(key, 8)
        z = jax.random.normal(ks[0], (N, H), dtype=jnp.float32)
        edge_index = jax.random.randint(ks[1], (2, E), 0, N, dtype=jnp.int64)
        edge_weight = jax.random.uniform(ks[2], (E,), dtype=jnp.float32)
        s = 1.0 / np.sqrt(H)
        weight = jax.random.uniform(ks[3], (L, H, H), minval=-s, maxval=s, dtype=jnp.float32)
        w_ih = jax.random.uniform(ks[4], (3 * H, H), minval=-s, maxval=s, dtype=jnp.float32)
        w_hh = jax.random.uniform(ks[5], (3 * H, H), minval=-s, maxval=s, dtype=jnp.float32)
        b_ih = jax.random.uniform(ks[6], (3 * H,), minval=-s, maxval=s, dtype=jnp.float32)
        b_hh = jax.random.uniform(ks[7], (3 * H,), minval=-s, maxval=s, dtype=jnp.float32)
        return {'z': z, 'edge_weight': edge_weight, 'weight': weight, 'w_ih': w_ih, 'w_hh': w_hh, 'b_ih': b_ih, 'b_hh': b_hh, 'edge_index': edge_index}
    _L0_gnn_all = _L0_gnn_setup()
    _L0_gnn_in = {k: v for k, v in _L0_gnn_all.items() if k in ('weight', 'w_ih', 'w_hh', 'b_ih', 'b_hh')}
    del _L0_gnn_all

    def _L1_gnn_setup():
        import jax, jax.numpy as jnp
        import numpy as np
        N_NODES = 6250
        N_EDGES = 100000
        D = 128
        NUM_LAYERS = 3

        def _gin_layer(x, src, dst, W, b):
            agg = jax.ops.segment_sum(x[src], dst, num_segments=N_NODES)
            h = (x + agg) @ W.T + b
            return jax.nn.relu(h)
        key = jax.random.key(seed)
        ks = jax.random.split(key, 2 + 2 * NUM_LAYERS)
        x = jax.random.normal(ks[0], (N_NODES, D), dtype=jnp.float32)
        edge_index = jax.random.randint(ks[1], (2, N_EDGES), 0, N_NODES, dtype=jnp.int64)
        scale = 1.0 / np.sqrt(D)
        inp = {'x': x, 'edge_index': edge_index}
        for i in range(NUM_LAYERS):
            inp[f'W{i}'] = jax.random.uniform(ks[2 + 2 * i], (D, D), dtype=jnp.float32, minval=-scale, maxval=scale)
            inp[f'b{i}'] = jax.random.uniform(ks[3 + 2 * i], (D,), dtype=jnp.float32, minval=-scale, maxval=scale)
        return inp
    _L1_gnn_all = _L1_gnn_setup()
    _L1_gnn_in = {k: v for k, v in _L1_gnn_all.items() if k in ('W0', 'b0', 'W1', 'b1', 'W2', 'b2')}
    del _L1_gnn_all
    return {'x': x, 'src': src, 'dst': dst, 'edge_weight': edge_weight, 'L0_gnn_weight': _L0_gnn_in['weight'], 'L0_gnn_w_ih': _L0_gnn_in['w_ih'], 'L0_gnn_w_hh': _L0_gnn_in['w_hh'], 'L0_gnn_b_ih': _L0_gnn_in['b_ih'], 'L0_gnn_b_hh': _L0_gnn_in['b_hh'], 'L1_gnn_W0': _L1_gnn_in['W0'], 'L1_gnn_b0': _L1_gnn_in['b0'], 'L1_gnn_W1': _L1_gnn_in['W1'], 'L1_gnn_b1': _L1_gnn_in['b1'], 'L1_gnn_W2': _L1_gnn_in['W2'], 'L1_gnn_b2': _L1_gnn_in['b2']}

def reference(x, src, dst, edge_weight, L0_gnn_weight, L0_gnn_w_ih, L0_gnn_w_hh, L0_gnn_b_ih, L0_gnn_b_hh, L1_gnn_W0, L1_gnn_b0, L1_gnn_W1, L1_gnn_b1, L1_gnn_W2, L1_gnn_b2):
    import jax
    import jax.numpy as jnp

    def _L0_gnn_ref(z, edge_weight, weight, w_ih, w_hh, b_ih, b_hh, edge_index):
        import jax, jax.numpy as jnp
        import numpy as np
        N = 6250
        E = 100000
        H = 128
        L = 3

        def _gru_cell(m, h, w_ih, w_hh, b_ih, b_hh):
            gi = m @ w_ih.T + b_ih
            gh = h @ w_hh.T + b_hh
            i_r, i_z, i_n = jnp.split(gi, 3, axis=-1)
            h_r, h_z, h_n = jnp.split(gh, 3, axis=-1)
            r = jax.nn.sigmoid(i_r + h_r)
            zg = jax.nn.sigmoid(i_z + h_z)
            n = jnp.tanh(i_n + r * h_n)
            return (1.0 - zg) * n + zg * h
        src = edge_index[0]
        dst = edge_index[1]
        x = z
        for l in range(L):
            m = x @ weight[l]
            msg = m[src] * edge_weight[:, None]
            agg = jax.ops.segment_sum(msg, dst, num_segments=N)
            x = _gru_cell(agg, x, w_ih, w_hh, b_ih, b_hh)
        return x

    def _L1_gnn_ref(x, edge_index, W0, b0, W1, b1, W2, b2):
        import jax, jax.numpy as jnp
        import numpy as np
        N_NODES = 6250
        N_EDGES = 100000
        D = 128
        NUM_LAYERS = 3

        def _gin_layer(x, src, dst, W, b):
            agg = jax.ops.segment_sum(x[src], dst, num_segments=N_NODES)
            h = (x + agg) @ W.T + b
            return jax.nn.relu(h)
        src, dst = (edge_index[0], edge_index[1])
        for W, b in ((W0, b0), (W1, b1), (W2, b2)):
            x = _gin_layer(x, src, dst, W, b)
        return x
    edge_index = jnp.stack([src, dst])
    x = _layernorm(x + _L0_gnn_ref(x, edge_weight, L0_gnn_weight, L0_gnn_w_ih, L0_gnn_w_hh, L0_gnn_b_ih, L0_gnn_b_hh, edge_index), axis=-1)
    x = _layernorm(x + _L1_gnn_ref(x, edge_index, L1_gnn_W0, L1_gnn_b0, L1_gnn_W1, L1_gnn_b1, L1_gnn_W2, L1_gnn_b2), axis=-1)
    return x

_drawn_inputs = setup_inputs


def setup_inputs(seed=0):
    import zlib

    import numpy as np

    out = dict(_drawn_inputs(seed))
    spreads = {}
    factors = {'L1_gnn_b0': 3.709, 'L1_gnn_b1': 34.591, 'L1_gnn_b2': 200.0}
    for name, (base, spread) in spreads.items():
        noise = np.random.default_rng([zlib.crc32(name.encode()), seed]).standard_normal(out[name].shape)
        drawn = base * np.exp(spread * noise) if base else spread * noise
        out[name] = jnp.asarray(drawn.astype(out[name].dtype))
    for name, factor in factors.items():
        out[name] = (out[name] * factor).astype(out[name].dtype)
    return out
```

```python
from contextlib import ExitStack

import concourse.bass as bass
from concourse import mybir

F32 = mybir.dt.float32
I32 = mybir.dt.int32
ALU = mybir.AluOpType
ACT = mybir.ActivationFunctionType

P = 128
N_NODES = 6250
N_EDGES = 200000
N_LAYERS = 3
EPS = 1e-5
TILES = -(-N_NODES // P)
NODES = TILES * P
FULL = N_NODES // P
TAIL = N_NODES - FULL * P
GROUPS = 14
GW = NODES // GROUPS
SUB = GW // 2
STRIPS = NODES // SUB
SLABS = 7
SH = TILES // SLABS
ROW = TILES * SUB
SIZE = STRIPS * P * ROW
EB = 125
BLOCKS = N_EDGES // EB
CHUNK = 4
CHUNKS = [(c, min(CHUNK, TILES - c)) for c in range(0, TILES, CHUNK)]
NC = len(CHUNKS)


def gnn_program(nc, x, src, dst, edge_weight, gnn_w, w_ih, w_hh, b_ih, b_hh,
                W0, b0, W1, b1, W2, b2, out):
    ctx = ExitStack()
    with ctx:
        def sb(name, shape, dt=F32):
            return ctx.enter_context(nc.sbuf_tensor(name, shape, dt))

        def sem(name):
            return ctx.enter_context(nc.semaphore(name))

        adj_w = nc.dram_tensor("adj_w", [SIZE + P], F32).ap()
        adj_c = nc.dram_tensor("adj_c", [SIZE + P], F32).ap()

        def strips(adj):
            return adj[0:SIZE].rearrange("(u p h c) -> p u h c", p=P, h=TILES, c=SUB)

        xT = sb("xT", [P, NODES])
        resT = sb("resT", [P, NODES])
        Y = sb("Y", [P, TILES, P])
        ring = sb("ring", [P, SLABS, 2, SH, SUB])
        ident = sb("ident", [P, P])
        aggS = sb("aggS", [P, 2, GW])
        r_t = sb("r_t", [P, GW])
        z_t = sb("z_t", [P, GW])
        t_t = sb("t_t", [P, GW])
        n_t = sb("n_t", [P, GW])
        w_raw = sb("w_raw", [P, 9, P])
        wT = sb("wT", [P, 9, P])
        gw = sb("gw", [P, N_LAYERS, P])
        wcur = sb("wcur", [P, P])
        bih = sb("bih", [P, 3])
        bhh = sb("bhh", [P, 3])
        brz = sb("brz", [P, 2])
        bg = sb("bg", [P, 3])
        bcur = sb("bcur", [P, 1])
        eps_t = sb("eps_t", [P, 1])
        stats = sb("stats", [P, CHUNK, 6])
        mv = sb("mv", [P, 2, CHUNK, 2])
        std = sb("std", [P, 2, CHUNK])
        rstd = sb("rstd", [P, 2, CHUNK])
        src_c = sb("src_c", [EB, 1], I32)
        dst_c = sb("dst_c", [EB, 1], I32)
        src_r = sb("src_r", [EB, EB], I32)
        dst_r = sb("dst_r", [EB, EB], I32)
        w_r = sb("w_r", [EB, EB])
        same = sb("same", [EB, EB])
        both = sb("both", [EB, EB])
        junk = sb("junk", [EB, EB])
        earlier = sb("earlier", [EB, EB])
        thresholds = sb("thresholds", [EB, STRIPS - 1])
        tjunk = sb("tjunk", [EB, STRIPS - 1])
        row_id = sb("row_id", [EB, 1])
        w_sum = sb("w_sum", [EB, 1])
        count = sb("count", [EB, 1])
        n_before = sb("n_before", [EB, 1])
        lo_i = sb("lo_i", [EB, 1], I32)
        hi_i = sb("hi_i", [EB, 1], I32)
        scal = sb("scal", [EB, 8])
        part_i = sb("part_i", [EB, 2], I32)
        cell = sb("cell", [EB, 1], I32)
        ps = ctx.enter_context(nc.psum_tensor("ps", [P, 8, 512], F32))

        s_const = sem("s_const")
        s_in = sem("s_in")
        s_zfill = sem("s_zfill")
        s_zero = sem("s_zero")
        s_ld = [sem(f"s_ld{i}") for i in range(5)]
        s_bv = sem("s_bv")
        s_scw = sem("s_scw")
        s_scc = sem("s_scc")
        s_scattered = sem("s_scattered")
        s_slab = [sem(f"s_slab{s}") for s in range(SLABS)]
        s_used = sem("s_used")
        s_setp = sem("s_setp")
        s_setv = sem("s_setv")
        s_yp = sem("s_yp")
        s_ye = sem("s_ye")
        s_agg = sem("s_agg")
        s_evac = sem("s_evac")
        s_gate = sem("s_gate")
        s_rz = sem("s_rz")
        s_gv = sem("s_gv")
        s_n = sem("s_n")
        s_cur = sem("s_cur")
        s_lnv = sem("s_lnv")
        s_lnp = sem("s_lnp")
        s_lna = sem("s_lna")
        s_lnb = sem("s_lnb")
        s_lnc = sem("s_lnc")
        s_lnd = sem("s_lnd")
        s_out = sem("s_out")
        s_mark_dve = sem("s_mark_dve")
        s_mark_pool = sem("s_mark_pool")
        s_mark_pe = sem("s_mark_pe")

        GV = 5
        BV = 19
        N_IN = 17
        N_CONST = 7
        START = 1
        FREE = 2
        LN_STEPS = sum(1 + 3 * n + 1 for _, n in CHUNKS)
        SET0 = 1
        SET_ALL = SET0 + NC + 3 + 1

        LN_TAIL = []
        total = 0
        for _, n in CHUNKS:
            total += 3 * n + 1
            LN_TAIL.append(total)
        ring_flat = ring[:, :, :, :, :].rearrange("p s u h c -> p (s u h c)")

        def tile_cols(t, n=1):
            return slice(t * P, (t + n) * P)

        block = ctx.enter_context(nc.Block())

        @block.sync
        def _(sp):
            sp.wait_ge(s_setv, 1)
            sp.dma_start(Y[:, 0:FULL, :], x[0:FULL * P, :].rearrange("(t p) f -> p t f", p=P)).then_inc(s_in, 16)
            sp.dma_start(Y[0:TAIL, FULL, :], x[FULL * P:N_NODES, :]).then_inc(s_in, 16)
            sp.dma_start(w_raw[:, 0:3, :], w_ih.rearrange("(c p) f -> p c f", p=P)).then_inc(s_in, 16)
            sp.dma_start(w_raw[:, 3:6, :], w_hh.rearrange("(c p) f -> p c f", p=P)).then_inc(s_in, 16)
            for k, w in enumerate((W0, W1, W2)):
                sp.dma_start(w_raw[:, 6 + k, :], w).then_inc(s_in, 16)
            sp.dma_start(gw[:, :, :], gnn_w.rearrange("l i o -> i l o")).then_inc(s_in, 16)
            sp.wait_ge(s_zfill, 1)
            for adj in (adj_w, adj_c):
                for u in range(STRIPS):
                    sp.dma_start(adj[u * P * ROW:(u + 1) * P * ROW].rearrange("(p e) -> p e", p=P),
                                 ring_flat[:, 0:ROW]).then_inc(s_zero, 16)
            with sp.Fori(0, BLOCKS) as b:
                edges = bass.ds(b * EB, EB)
                sp.wait_ge(s_bv, START + BV * b)
                cols = [(src_c, src), (dst_c, dst)]
                for k, (t, a) in enumerate(cols):
                    sp.dma_start(t[:, :], a[edges].rearrange("(p o) -> p o", o=1)).then_inc(s_ld[k], 16)
                for k, (t, a) in enumerate(((src_r, src), (dst_r, dst), (w_r, edge_weight))):
                    sp.dma_start(t[:, :], a[edges].rearrange("(o e) -> o e", o=1).to_broadcast([EB, EB]))\
                      .then_inc(s_ld[2 + k], 16)
            sp.wait_ge(s_scattered, START + BLOCKS)

            def slabs(adj, g, n):
                for s in range(SLABS):
                    sp.wait_ge(s_used, SLABS * n + s + 1)
                    sp.dma_start(ring[:, s, :, :, :],
                                 strips(adj)[:, bass.ds(2 * g, 2), s * SH:(s + 1) * SH, :]).then_inc(s_slab[s], 16)

            for net, adj in enumerate((adj_w, adj_c)):
                with sp.Fori(0, N_LAYERS) as l:
                    with sp.Fori(0, GROUPS) as g:
                        slabs(adj, g, (net * N_LAYERS + l) * GROUPS + g)
            sp.wait_ge(s_lnv, LN_STEPS * 2)
            sp.dma_start(out[0:FULL * P, :].rearrange("(t p) f -> p t f", p=P), Y[:, 0:FULL, :]).then_inc(s_out, 16)
            sp.dma_start(out[FULL * P:N_NODES, :], Y[0:TAIL, FULL, :]).then_inc(s_out, 16)
            sp.wait_ge(s_out, 32)

        @block.gpsimd
        def _(pool):
            pool.memset(ident[:, :], 0.0).then_inc(s_const, 1)
            pool.memset(earlier[:, :], 1.0).then_inc(s_const, 1)
            pool.wait_ge(s_const, 2)
            pool.affine_select(out=ident[:, :], in_=ident[:, :], compare_op=ALU.not_equal, fill=1.0,
                               base=0, pattern=[[-1, P]], channel_multiplier=1).then_inc(s_const, 1)
            pool.affine_select(out=earlier[:, :], in_=earlier[:, :], compare_op=ALU.is_gt, fill=0.0,
                               base=0, pattern=[[-1, EB]], channel_multiplier=1).then_inc(s_const, 1)
            pool.iota(thresholds[:, :], pattern=[[SUB, STRIPS - 1]], base=SUB, channel_multiplier=0,
                      allow_small_or_imprecise_dtypes=True).then_inc(s_const, 1)
            pool.iota(row_id[:, :], pattern=[[0, 1]], base=0, channel_multiplier=1,
                      allow_small_or_imprecise_dtypes=True).then_inc(s_const, 1)
            pool.memset(eps_t[:, :], EPS).then_inc(s_const, 1)
            pool.wait_ge(s_zero, 16 * 2 * STRIPS)
            with pool.Fori(0, BLOCKS) as b:
                pool.wait_ge(s_bv, START + BV * (b + 1))
                pool.sem_inc(s_mark_pool, 1)
                for adj, val, s in ((adj_w, w_sum, s_scw), (adj_c, count, s_scc)):
                    pool.indirect_dma_start(out=adj.rearrange("(e o) -> e o", o=1),
                                            out_offset=bass.IndirectOffsetOnAxis(ap=cell[:, 0:1], axis=0),
                                            in_=val[:, :], in_offset=None, compute_op=ALU.add).then_inc(s, 16)
                pool.wait_ge(s_scw, 16 * (b + 1))
                pool.wait_ge(s_scc, 16 * (b + 1))
                pool.sem_inc(s_scattered, 1)

        @block.tensor
        def _(pe):
            pe.sem_inc(s_used, SLABS)
            pe.sem_inc(s_evac, FREE)
            pe.sem_inc(s_gate, FREE)
            for s in (s_gv, s_rz, s_n, s_ye, s_bv, s_scattered):
                pe.sem_inc(s, START)
            pe.wait_ge(s_const, N_CONST)
            pe.wait_ge(s_in, 16 * N_IN)
            for j, (c, n) in enumerate(CHUNKS):
                if j >= 2:
                    pe.wait_ge(s_setv, SET0 + j - 1)
                for k in range(n):
                    mm = pe.transpose(ps[:, 6 + j % 2, k * P:(k + 1) * P], Y[:, c + k, :], ident[:, :])
                mm.then_inc(s_setp, 1)
            for j in range(9):
                mm = pe.transpose(ps[:, j // 4, (j % 4) * P:(j % 4 + 1) * P], w_raw[:, j, :], ident[:, :])
            mm.then_inc(s_setp, 1)
            pe.wait_ge(s_setv, SET_ALL)

            def node_major(layer, w):
                for j, (c, n) in enumerate(CHUNKS):
                    pe.wait_ge(s_ye, START + NC * layer + max(j - 1, 0))
                    for k in range(n):
                        mm = pe.matmul(ps[:, 6 + j % 2, k * P:(k + 1) * P], xT[:, tile_cols(c + k)], w,
                                       start=True, stop=True)
                    mm.then_inc(s_yp, 1)
                pe.wait_ge(s_ye, START + NC * layer + NC)
                pe.sem_inc(s_mark_pe, 1)

            def aggregate(n, bank, last=True):
                pe.wait_ge(s_evac, n + 1)
                for s in range(SLABS):
                    pe.wait_ge(s_slab[s], 16 * (n + 1))
                    for k in range(SH):
                        h = s * SH + k
                        mm = pe.matmul(ps[:, bank, 0:GW], Y[:, h, :], ring[:, s, :, k, :],
                                       start=(h == 0), stop=(last and h == TILES - 1))
                    mm.then_inc(s_used, 1)

            def gates(n, par, g):
                xg = xT[:, bass.ds(g * GW, GW)]
                pe.wait_ge(s_evac, FREE + n + 1)
                pe.wait_ge(s_rz, START + 2 * n)
                pe.wait_ge(s_gv, START + GV * n)
                for bank, c in ((2, 0), (3, 1)):
                    pe.matmul(ps[:, bank, 0:GW], wT[:, c, :], aggS[:, par, :], start=True, stop=False)
                    pe.matmul(ps[:, bank, 0:GW], wT[:, 3 + c, :], xg, start=False, stop=True)
                pe.matmul(ps[:, 4, 0:GW], wT[:, 2, :], aggS[:, par, :], start=True, stop=True)
                pe.matmul(ps[:, 5, 0:GW], wT[:, 5, :], xg, start=True, stop=True).then_inc(s_gate, 1)

            with pe.Fori(0, N_LAYERS) as l:
                n0 = l * GROUPS
                pe.wait_ge(s_gv, START + GV * n0)
                node_major(l, gw[:, bass.ds(l, 1), :].rearrange("p o f -> p (o f)"))
                aggregate(n0, 0)
                with pe.Fori(0, GROUPS // 2 - 1) as i:
                    n = n0 + 2 * i
                    aggregate(n + 1, 1)
                    gates(n, 0, 2 * i)
                    aggregate(n + 2, 0)
                    gates(n + 1, 1, 2 * i + 1)
                aggregate(n0 + GROUPS - 1, 1)
                gates(n0 + GROUPS - 2, 0, GROUPS - 2)
                gates(n0 + GROUPS - 1, 1, GROUPS - 1)

            def ln_forward(which):
                for j, (c, n) in enumerate(CHUNKS):
                    pe.wait_ge(s_lnv, which * LN_STEPS + NC + (LN_TAIL[j - 2] if j >= 2 else 0))
                    for k in range(n):
                        mm = pe.transpose(ps[:, 6 + j % 2, k * P:(k + 1) * P], xT[:, tile_cols(c + k)], ident[:, :])
                    mm.then_inc(s_lnp, 1)

            ln_forward(0)
            for j, (c, n) in enumerate(CHUNKS):
                pe.wait_ge(s_lnv, NC + LN_TAIL[j])
                if j >= 2:
                    pe.wait_ge(s_lnc, j - 1)
                    pe.wait_ge(s_lnd, j - 1)
                for k in range(n):
                    mm = pe.transpose(ps[:, 4 + j % 2, k * P:(k + 1) * P], Y[:, c + k, :], ident[:, :])
                mm.then_inc(s_lnb, 1)
            pe.wait_ge(s_lnc, NC)

            with pe.Fori(0, N_LAYERS) as l:
                n0 = (N_LAYERS + l) * GROUPS
                pe.wait_ge(s_evac, FREE + n0)
                pe.wait_ge(s_cur, 2 * (l + 1))
                node_major(N_LAYERS + l, wcur[:, :])
                with pe.Fori(0, GROUPS // 2) as i:
                    for par in range(2):
                        n = n0 + 2 * i + par
                        aggregate(n, par, last=False)
                        pe.matmul(ps[:, par, 0:GW], wcur[:, :], xT[:, bass.ds((2 * i + par) * GW, GW)],
                                  start=False, stop=True).then_inc(s_agg, 1)
            pe.wait_ge(s_evac, FREE + 2 * N_LAYERS * GROUPS)
            ln_forward(1)

        @block.scalar
        def _(act):
            for t, b in ((bih, b_ih), (bhh, b_hh)):
                for c in range(3):
                    act.dma_start(t[:, c:c + 1], b[c * P:(c + 1) * P].rearrange("(p o) -> p o", o=1))\
                       .then_inc(s_in, 16)
            for k, b in enumerate((b0, b1, b2)):
                act.dma_start(bg[:, k:k + 1], b.rearrange("(p o) -> p o", o=1)).then_inc(s_in, 16)

            def evac(n, par):
                act.wait_ge(s_used, SLABS * (n + 2))
                act.wait_ge(s_gate, n + 1)
                act.activation(aggS[:, par, :], ps[:, par, 0:GW], ACT.Copy).then_inc(s_evac, 1)

            def update(n):
                act.wait_ge(s_gate, FREE + n + 1)
                act.wait_ge(s_gv, START + GV * n)
                act.activation(r_t[:, :], ps[:, 2, 0:GW], ACT.Sigmoid, bias=brz[:, 0:1]).then_inc(s_rz, 1)
                act.activation(z_t[:, :], ps[:, 3, 0:GW], ACT.Sigmoid, bias=brz[:, 1:2]).then_inc(s_rz, 1)
                act.wait_ge(s_gv, START + GV * n + 2)
                act.activation(n_t[:, :], t_t[:, :], ACT.Tanh).then_inc(s_n, 1)

            act.wait_ge(s_setv, SET_ALL)
            with act.Fori(0, N_LAYERS) as l:
                n0 = l * GROUPS
                evac(n0, 0)
                with act.Fori(0, GROUPS // 2 - 1) as i:
                    n = n0 + 2 * i
                    evac(n + 1, 1)
                    update(n)
                    evac(n + 2, 0)
                    update(n + 1)
                evac(n0 + GROUPS - 1, 1)
                update(n0 + GROUPS - 2)
                update(n0 + GROUPS - 1)

            def ln_std(which):
                done = 0
                for j, (c, n) in enumerate(CHUNKS):
                    act.wait_ge(s_lnv, which * LN_STEPS + NC + (LN_TAIL[j - 1] if j else 0) + 2 * n)
                    act.activation(std[:, j % 2, 0:n], mv[:, j % 2, 0:n, 1:2].rearrange("p t o -> p (t o)"), ACT.Sqrt,
                                   bias=eps_t[:, 0:1]).then_inc(s_lna, 1)

            ln_std(0)
            for j, (c, n) in enumerate(CHUNKS):
                act.wait_ge(s_lnc, j + 1)
                act.activation(resT[:, tile_cols(c, n)], ps[:, 4 + j % 2, 0:n * P], ACT.Copy).then_inc(s_lnd, 1)
            with act.Fori(0, N_LAYERS) as l:
                act.wait_ge(s_cur, 2 * (l + 1))
                with act.Fori(0, GROUPS // 2) as i:
                    for par in range(2):
                        g = 2 * i + par
                        act.wait_ge(s_agg, l * GROUPS + g + 1)
                        act.activation(xT[:, bass.ds(g * GW, GW)], ps[:, par, 0:GW], ACT.Relu, bias=bcur[:, 0:1])\
                           .then_inc(s_evac, 1)
            ln_std(1)

        @block.vector
        def _(dve):
            dve.memset(Y[:, FULL, :], 0.0).then_inc(s_setv, 1)
            dve.memset(ring_flat[:, 0:ROW], 0.0).then_inc(s_zfill, 1)
            for j, (c, n) in enumerate(CHUNKS):
                dve.wait_ge(s_setp, j + 1)
                dve.tensor_copy(xT[:, tile_cols(c, n)], ps[:, 6 + j % 2, 0:n * P]).then_inc(s_setv, 1)
            dve.wait_ge(s_setp, NC + 1)
            for j in range(3):
                n = min(4, 9 - 4 * j)
                dve.tensor_copy(wT[:, 4 * j:4 * j + n, :], ps[:, j, 0:n * P].rearrange("p (c f) -> p c f", f=P))\
                   .then_inc(s_setv, 1)
            dve.tensor_tensor(brz[:, :], bih[:, 0:2], bhh[:, 0:2], ALU.add).then_inc(s_setv, 1)
            dve.wait_ge(s_setv, SET_ALL)
            dve.tensor_copy(resT[:, :], xT[:, :]).then_inc(s_setv, 1)
            dve.wait_ge(s_setv, SET_ALL + 1)

            dve.wait_ge(s_const, N_CONST)
            with dve.Fori(0, BLOCKS) as b:
                for s in s_ld:
                    dve.wait_ge(s, 16 * (b + 1))
                dve.wait_ge(s_scattered, START + b)
                done = [0]

                def step(ins):
                    done[0] += 1
                    ins.then_inc(s_bv, 1)
                    if done[0] < BV:
                        dve.wait_ge(s_bv, START + BV * b + done[0])

                strip, major, minor, col, rep, keep, m1, m2 = (scal[:, i:i + 1] for i in range(8))
                step(dve.tensor_scalar(same[:, :], src_r[:, :], src_c[:, 0:1], None, ALU.is_equal))
                step(dve.scalar_tensor_tensor(out=both[:, :], in0=dst_r[:, :], scalar=dst_c[:, 0:1], in1=same[:, :],
                                              op0=ALU.is_equal, op1=ALU.mult))
                for other, acc in ((w_r, w_sum), (both, count), (earlier, n_before)):
                    step(dve.tensor_tensor_reduce(junk[:, :], both[:, :], other[:, :], 1.0, 0.0, ALU.mult, ALU.add,
                                                  acc[:, :]))
                step(dve.tensor_scalar(lo_i[:, :], src_c[:, :], P - 1, None, ALU.bitwise_and))
                step(dve.tensor_scalar(hi_i[:, :], src_c[:, :], 7, None, ALU.logical_shift_right))
                step(dve.tensor_scalar(m1, dst_c[:, :], 1.0, None, ALU.mult))
                step(dve.tensor_scalar(tjunk[:, :], thresholds[:, :], m1, 0.0, ALU.is_le, ALU.add,
                                       accum_out=strip))
                step(dve.scalar_tensor_tensor(out=major, in0=strip, scalar=float(P), in1=lo_i[:, :],
                                              op0=ALU.mult, op1=ALU.add))
                step(dve.scalar_tensor_tensor(out=col, in0=strip, scalar=float(-SUB), in1=dst_c[:, :],
                                              op0=ALU.mult, op1=ALU.add))
                step(dve.scalar_tensor_tensor(out=minor, in0=hi_i[:, :], scalar=float(SUB), in1=col,
                                              op0=ALU.mult, op1=ALU.add))
                step(dve.tensor_scalar(rep, n_before[:, :], 0.0, None, ALU.is_gt))
                step(dve.tensor_scalar(keep, n_before[:, :], 0.0, None, ALU.is_equal))
                step(dve.tensor_scalar(m1, major, float(ROW), keep, ALU.mult, ALU.mult))
                step(dve.scalar_tensor_tensor(out=part_i[:, 0:1], in0=rep, scalar=float(SIZE), in1=m1,
                                              op0=ALU.mult, op1=ALU.add))
                step(dve.tensor_scalar(m2, minor, keep, None, ALU.mult))
                step(dve.scalar_tensor_tensor(out=part_i[:, 1:2], in0=rep, scalar=row_id[:, 0:1], in1=m2,
                                              op0=ALU.mult, op1=ALU.add))
                dve.sem_inc(s_mark_dve, 1)
                step(dve.tensor_tensor(cell[:, :], part_i[:, 0:1], part_i[:, 1:2], ALU.add))
                assert done[0] == BV

            def take_node_major(layer):
                for j, (c, n) in enumerate(CHUNKS):
                    dve.wait_ge(s_yp, NC * layer + j + 1)
                    dve.tensor_copy(Y[:, c:c + n, :], ps[:, 6 + j % 2, 0:n * P].rearrange("p (c f) -> p c f", f=P))\
                       .then_inc(s_ye, 1)

            with dve.Fori(0, N_LAYERS) as l:
                take_node_major(l)
                with dve.Fori(0, GROUPS) as g:
                    n = l * GROUPS + g
                    xg = xT[:, bass.ds(g * GW, GW)]
                    dve.wait_ge(s_gate, FREE + n + 1)
                    dve.wait_ge(s_n, START + n)
                    dve.wait_ge(s_rz, START + 2 * n + 1)
                    dve.scalar_tensor_tensor(out=t_t[:, :], in0=ps[:, 5, 0:GW], scalar=bhh[:, 2:3], in1=r_t[:, :],
                                             op0=ALU.add, op1=ALU.mult).then_inc(s_gv, 1)
                    dve.wait_ge(s_gv, START + GV * n + 1)
                    dve.scalar_tensor_tensor(out=t_t[:, :], in0=ps[:, 4, 0:GW], scalar=bih[:, 2:3], in1=t_t[:, :],
                                             op0=ALU.add, op1=ALU.add).then_inc(s_gv, 1)
                    dve.wait_ge(s_n, START + n + 1)
                    dve.tensor_tensor(xg, xg, n_t[:, :], ALU.subtract).then_inc(s_gv, 1)
                    dve.wait_ge(s_gv, START + GV * n + 3)
                    dve.wait_ge(s_rz, START + 2 * n + 2)
                    dve.tensor_tensor(xg, xg, z_t[:, :], ALU.mult).then_inc(s_gv, 1)
                    dve.wait_ge(s_gv, START + GV * n + 4)
                    dve.tensor_tensor(xg, xg, n_t[:, :], ALU.add).then_inc(s_gv, 1)

            def layer_norm(which):
                v0 = which * LN_STEPS
                for j, (c, n) in enumerate(CHUNKS):
                    dve.tensor_tensor(xT[:, tile_cols(c, n)], xT[:, tile_cols(c, n)], resT[:, tile_cols(c, n)],
                                      ALU.add).then_inc(s_lnv, 1)
                v = v0 + NC
                for j, (c, n) in enumerate(CHUNKS):
                    dve.wait_ge(s_lnp, which * NC + j + 1)
                    node = ps[:, 6 + j % 2, 0:n * P].rearrange("p (t f) -> p t f", f=P)
                    for k in range(n):
                        dve.bn_stats(stats[:, k, :], node[:, k, :]).then_inc(s_lnv, 1)
                    dve.wait_ge(s_lnv, v + n)
                    for k in range(n):
                        dve.bn_aggr(mv[:, j % 2, k, :], stats[:, k, :]).then_inc(s_lnv, 1)
                    dve.wait_ge(s_lna, which * NC + j + 1)
                    dve.reciprocal(rstd[:, j % 2, 0:n], std[:, j % 2, 0:n]).then_inc(s_lnv, 1)
                    dve.wait_ge(s_lnv, v + 2 * n + 1)
                    for k in range(n):
                        dve.tensor_scalar(Y[:, c + k, :], node[:, k, :], mv[:, j % 2, k, 0:1],
                                          rstd[:, j % 2, k:k + 1], ALU.subtract, ALU.mult).then_inc(s_lnv, 1)
                    v += 3 * n + 1

            dve.wait_ge(s_gv, START + GV * N_LAYERS * GROUPS)
            layer_norm(0)
            for j, (c, n) in enumerate(CHUNKS):
                dve.wait_ge(s_lnb, j + 1)
                dve.tensor_copy(xT[:, tile_cols(c, n)], ps[:, 4 + j % 2, 0:n * P]).then_inc(s_lnc, 1)
            with dve.Fori(0, N_LAYERS) as l:
                dve.wait_ge(s_evac, FREE + (N_LAYERS + l) * GROUPS)
                dve.tensor_copy(wcur[:, :], wT[:, bass.ds(6 + l, 1), :].rearrange("p o f -> p (o f)")).then_inc(s_cur, 1)
                dve.tensor_copy(bcur[:, :], bg[:, bass.ds(l, 1)]).then_inc(s_cur, 1)
                take_node_major(N_LAYERS + l)
            dve.wait_ge(s_evac, FREE + 2 * N_LAYERS * GROUPS)
            dve.wait_ge(s_lnd, NC)
            layer_norm(1)


_INS = ['x', 'src', 'dst', 'edge_weight', 'L0_gnn_weight', 'L0_gnn_w_ih', 'L0_gnn_w_hh', 'L0_gnn_b_ih', 'L0_gnn_b_hh',
        'L1_gnn_W0', 'L1_gnn_b0', 'L1_gnn_W1', 'L1_gnn_b1', 'L1_gnn_W2', 'L1_gnn_b2']


def kernel(**inputs):
    import numpy as _np
    import concourse.bacc as _bacc
    from concourse import mybir as _mybir
    from concourse.bass_utils import run_bass_kernel_spmd as _run

    nc = _bacc.Bacc("TRN2", target_bir_lowering=False, num_devices=1)
    arrays, args = {}, []
    for name in _INS:
        a = _np.ascontiguousarray(inputs[name])
        arrays[f"in_{name}"] = a
        args.append(nc.dram_tensor(f"in_{name}", a.shape, _mybir.dt.from_np(a.dtype), kind="ExternalInput").ap())
    args.append(nc.dram_tensor("out_0", (N_NODES, P), _mybir.dt.float32, kind="ExternalOutput").ap())
    gnn_program(nc, *args)
    r = _run(nc, [arrays], core_ids=[0])
    return r.results[0]["out_0"]
```

```python
from contextlib import ExitStack

import concourse.bass as bass
from concourse import mybir

F32 = mybir.dt.float32
I32 = mybir.dt.int32
ALU = mybir.AluOpType
ACT = mybir.ActivationFunctionType

P = 128
N_NODES = 6250
N_EDGES = 200000
N_LAYERS = 3
EPS = 1e-5
TILES = -(-N_NODES // P)
NODES = TILES * P
FULL = N_NODES // P
TAIL = N_NODES - FULL * P
GROUPS = 14
GW = NODES // GROUPS
SUB = GW // 4
PARTS = GW // SUB
STRIPS = NODES // SUB
SLABS = 7
SH = TILES // SLABS
ROW = TILES * SUB
SIZE = STRIPS * P * ROW
WIN = 2
SLOTS = P
LANES = 112
GATHERS = NODES // WIN // LANES
WINDOWS = GATHERS * LANES
KEYS = WIN * TILES
BATCH = 8
STRIP_BATCHES = SUB // WIN // BATCH
STRIPS_PER_GATHER = WIN * LANES // SUB
BATCHES_PER_GATHER = STRIPS_PER_GATHER * STRIP_BATCHES
EB = 125
BLOCKS = N_EDGES // EB
CHUNK = 4
CHUNKS = [(c, min(CHUNK, TILES - c)) for c in range(0, TILES, CHUNK)]
NC = len(CHUNKS)


def gnn_program(nc, x, src, dst, edge_weight, gnn_w, w_ih, w_hh, b_ih, b_hh,
                W0, b0, W1, b1, W2, b2, out):
    ctx = ExitStack()
    with ctx:
        def sb(name, shape, dt=F32):
            return ctx.enter_context(nc.sbuf_tensor(name, shape, dt))

        def sem(name):
            return ctx.enter_context(nc.semaphore(name))

        adj_w = nc.dram_tensor("adj_w", [SIZE + P], F32).ap()
        adj_c = nc.dram_tensor("adj_c", [SIZE + P], F32).ap()

        def strip_rows(adj):
            return adj[0:SIZE].rearrange("(u p e) -> u p e", p=P, e=ROW)

        def strips(adj):
            return adj[0:SIZE].rearrange("(u p h c) -> p u h c", p=P, h=TILES, c=SUB)

        xT = sb("xT", [P, NODES])
        shared = sb("shared", [P, 3 * WINDOWS])
        columns = shared[:, :].rearrange("p (k w) -> p k w", k=3)
        resT = shared[:, 0:NODES]

        def gate_buffer(i):
            return shared[:, NODES + i * GW:NODES + (i + 1) * GW]

        Y = sb("Y", [P, TILES, P])
        ring = sb("ring", [P, SLABS, PARTS, SH, SUB])
        ident = sb("ident", [P, P])
        aggS = [gate_buffer(0), gate_buffer(1)]
        r_t, z_t, t_t, n_t = (gate_buffer(i) for i in range(2, 6))
        w_raw = sb("w_raw", [P, 9, P])
        wT = sb("wT", [P, 9, P])
        gw = sb("gw", [P, N_LAYERS, P])
        wcur = sb("wcur", [P, P])
        bih = sb("bih", [P, 3])
        bhh = sb("bhh", [P, 3])
        brz = sb("brz", [P, 2])
        bg = sb("bg", [P, 3])
        bcur = sb("bcur", [P, 1])
        eps_t = sb("eps_t", [P, 1])
        stats = sb("stats", [P, CHUNK, 6])
        mv = sb("mv", [P, 2, CHUNK, 2])
        std = sb("std", [P, 2, CHUNK])
        rstd = sb("rstd", [P, 2, CHUNK])
        firsts = nc.dram_tensor("firsts", [BLOCKS], I32).ap()
        bases = sb("bases", [LANES, GATHERS])
        n_blocks = sb("n_blocks", [LANES, GATHERS])
        in_block = sb("in_block", [LANES, GATHERS])
        block_i = sb("block_i", [LANES, GATHERS], I32)
        start_i = sb("start_i", [LANES, GATHERS], I32)
        covered = sb("covered", [LANES, 1])
        ones = sb("ones", [LANES, 1])
        flag = sb("flag", [1, 1], I32)
        iota_lo = sb("iota_lo", [P, P])
        iota_key = sb("iota_key", [P, KEYS])
        src_c = sb("src_c", [EB, 1], I32)
        dst_c = sb("dst_c", [EB, 1], I32)
        src_r = sb("src_r", [EB, EB], I32)
        dst_r = sb("dst_r", [EB, EB], I32)
        w_r = sb("w_r", [EB, EB])
        same = sb("same", [EB, EB])
        both = sb("both", [EB, EB])
        junk = sb("junk", [EB, EB])
        earlier = sb("earlier", [EB, EB])
        thresholds = sb("thresholds", [EB, STRIPS - 1])
        tjunk = sb("tjunk", [EB, STRIPS - 1])
        row_id = sb("row_id", [EB, 1])
        w_sum = sb("w_sum", [EB, 1])
        count = sb("count", [EB, 1])
        n_before = sb("n_before", [EB, 1])
        lo_i = sb("lo_i", [EB, 1], I32)
        hi_i = sb("hi_i", [EB, 1], I32)
        scal = sb("scal", [EB, 8])
        part_i = sb("part_i", [EB, 2], I32)
        cell = sb("cell", [EB, 1], I32)
        ps = ctx.enter_context(nc.psum_tensor("ps", [P, 8, 512], F32))

        s_const = sem("s_const")
        s_in = sem("s_in")
        s_zfill = sem("s_zfill")
        s_zero = sem("s_zero")
        s_ld = [sem(f"s_ld{i}") for i in range(5)]
        s_bv = sem("s_bv")
        s_scw = sem("s_scw")
        s_scc = sem("s_scc")
        s_scattered = sem("s_scattered")
        s_slab = [sem(f"s_slab{s}") for s in range(SLABS)]
        s_used = sem("s_used")
        s_setp = sem("s_setp")
        s_setv = sem("s_setv")
        s_yp = sem("s_yp")
        s_ye = sem("s_ye")
        s_agg = sem("s_agg")
        s_evac = sem("s_evac")
        s_gate = sem("s_gate")
        s_rz = sem("s_rz")
        s_gv = sem("s_gv")
        s_n = sem("s_n")
        s_cur = sem("s_cur")
        s_lnv = sem("s_lnv")
        s_lnp = sem("s_lnp")
        s_lna = sem("s_lna")
        s_lnb = sem("s_lnb")
        s_lnc = sem("s_lnc")
        s_lnd = sem("s_lnd")
        s_out = sem("s_out")
        s_first = sem("s_first")
        s_pv = sem("s_pv")
        s_rows = sem("s_rows")
        s_wdst = sem("s_wdst")
        s_wsrc = sem("s_wsrc")
        s_wwgt = sem("s_wwgt")
        s_cov = sem("s_cov")
        s_flag = sem("s_flag")
        s_colp = sem("s_colp")
        s_colv = sem("s_colv")
        s_hot = sem("s_hot")
        s_hotw = sem("s_hotw")
        s_bmm = sem("s_bmm")
        s_bev = sem("s_bev")
        s_strip = [sem("s_strip0"), sem("s_strip1")]
        s_sfree = sem("s_sfree")
        s_built = sem("s_built")
        s_mark_dve = sem("s_mark_dve")
        s_mark_pool = sem("s_mark_pool")
        s_mark_pe = sem("s_mark_pe")

        GV = 5
        BV = 19
        N_IN = 17
        N_CONST = 11
        AHEAD = 2
        PREP_CNT = 1 + GATHERS
        PREP_START = PREP_CNT + 2 + 4
        PREP_COVER = PREP_START + 4
        PREP_ALL = PREP_COVER + 4
        COL_BANKS = 3 * GATHERS // 4
        START = 1
        FREE = 2
        LN_STEPS = sum(1 + 3 * n + 1 for _, n in CHUNKS)
        SET0 = 1
        SET_ALL = SET0 + NC + 3 + 1

        LN_TAIL = []
        total = 0
        for _, n in CHUNKS:
            total += 3 * n + 1
            LN_TAIL.append(total)
        ring_flat = ring[:, :, :, :, :].rearrange("p s u h c -> p (s u h c)")

        def prep(i, dt=F32, width=GATHERS * SLOTS):
            v = ring_flat[0:LANES, i * GATHERS * SLOTS:i * GATHERS * SLOTS + width]
            return v if dt == F32 else v.bitcast(dt)

        def by_window(v, width=SLOTS):
            return v.rearrange("p (g e) -> p g e", e=width)

        strip_buf = ring_flat[:, 0:4 * ROW].rearrange("p (b k h c) -> p b k h c", b=2, k=2, h=TILES)
        y_flat = Y[:, :, :].rearrange("p t f -> p (t f)")
        hot_lo = y_flat[:, 0:2 * BATCH * P].rearrange("p (b w l) -> p b w l", b=2, w=BATCH)
        hot_key = y_flat[:, 2 * BATCH * P:2 * BATCH * (P + 2 * KEYS)].rearrange(
            "p (b w k x) -> p b w k x", b=2, w=BATCH, k=2)

        def tile_cols(t, n=1):
            return slice(t * P, (t + n) * P)

        block = ctx.enter_context(nc.Block())

        @block.sync
        def _(sp):
            sp.wait_ge(s_setv, 1)
            sp.dma_start(Y[:, 0:FULL, :], x[0:FULL * P, :].rearrange("(t p) f -> p t f", p=P)).then_inc(s_in, 16)
            sp.dma_start(Y[0:TAIL, FULL, :], x[FULL * P:N_NODES, :]).then_inc(s_in, 16)
            sp.dma_start(w_raw[:, 0:3, :], w_ih.rearrange("(c p) f -> p c f", p=P)).then_inc(s_in, 16)
            sp.dma_start(w_raw[:, 3:6, :], w_hh.rearrange("(c p) f -> p c f", p=P)).then_inc(s_in, 16)
            for k, w in enumerate((W0, W1, W2)):
                sp.dma_start(w_raw[:, 6 + k, :], w).then_inc(s_in, 16)
            sp.dma_start(gw[:, :, :], gnn_w.rearrange("l i o -> i l o")).then_inc(s_in, 16)
            with nc.allow_non_contiguous_dma(reason="one destination of each block"):
                sp.dma_start(firsts.rearrange("(b o) -> b o", o=1),
                             dst.rearrange("(b e) -> b e", e=EB)[:, 0:1]).then_inc(s_first, 16)
            sp.wait_ge(s_first, 16)
            sp.dma_start(prep(4, I32, BLOCKS), firsts.rearrange("(o b) -> o b", o=1).to_broadcast([LANES, BLOCKS]))\
              .then_inc(s_first, 16)
            sp.wait_ge(s_flag, 1)
            fits = sp.value_load(flag[0:1, 0:1], min_val=0, max_val=1)
            with sp.If(fits):
                with sp.Fori(0, GATHERS) as t:
                    for b in range(STRIPS_PER_GATHER):
                        u = STRIPS_PER_GATHER * t + b
                        sp.wait_ge(s_bev, 2 * AHEAD + 2 * STRIP_BATCHES * (u + 1))
                        for k, adj in enumerate((adj_w, adj_c)):
                            sp.dma_start(strip_rows(adj)[bass.ds(u, 1), :, :].rearrange("o p e -> (o p) e"),
                                         strip_buf[:, b, 1 - k, :, :].rearrange("p h c -> p (h c)"))\
                              .then_inc(s_strip[b], 16)
                        sp.wait_ge(s_strip[b], 32 * (t + 1))
                        sp.sem_inc(s_sfree, 1)
            with sp.Else():
                sp.wait_ge(s_zfill, 1)
                for adj in (adj_w, adj_c):
                    for u in range(STRIPS):
                        sp.dma_start(adj[u * P * ROW:(u + 1) * P * ROW].rearrange("(p e) -> p e", p=P),
                                     ring_flat[:, 0:ROW]).then_inc(s_zero, 16)
                with sp.Fori(0, BLOCKS) as b:
                    edges = bass.ds(b * EB, EB)
                    sp.wait_ge(s_bv, START + BV * b)
                    cols = [(src_c, src), (dst_c, dst)]
                    for k, (t, a) in enumerate(cols):
                        sp.dma_start(t[:, :], a[edges].rearrange("(p o) -> p o", o=1)).then_inc(s_ld[k], 16)
                    for k, (t, a) in enumerate(((src_r, src), (dst_r, dst), (w_r, edge_weight))):
                        sp.dma_start(t[:, :], a[edges].rearrange("(o e) -> o e", o=1).to_broadcast([EB, EB]))\
                          .then_inc(s_ld[2 + k], 16)
                sp.wait_ge(s_scattered, START + BLOCKS)
            sp.sem_inc(s_built, 1)

            def slabs(adj, g, n):
                for s in range(SLABS):
                    sp.wait_ge(s_used, SLABS * n + s + 1)
                    sp.dma_start(ring[:, s, :, :, :],
                                 strips(adj)[:, bass.ds(PARTS * g, PARTS), s * SH:(s + 1) * SH, :]).then_inc(s_slab[s], 16)

            for net, adj in enumerate((adj_w, adj_c)):
                with sp.Fori(0, N_LAYERS) as l:
                    with sp.Fori(0, GROUPS) as g:
                        slabs(adj, g, (net * N_LAYERS + l) * GROUPS + g)
            sp.wait_ge(s_lnv, LN_STEPS * 2)
            sp.dma_start(out[0:FULL * P, :].rearrange("(t p) f -> p t f", p=P), Y[:, 0:FULL, :]).then_inc(s_out, 16)
            sp.dma_start(out[FULL * P:N_NODES, :], Y[0:TAIL, FULL, :]).then_inc(s_out, 16)
            sp.wait_ge(s_out, 32)

        @block.gpsimd
        def _(pool):
            pool.memset(ident[:, :], 0.0).then_inc(s_const, 1)
            pool.memset(earlier[:, :], 1.0).then_inc(s_const, 1)
            pool.wait_ge(s_const, 2)
            pool.affine_select(out=ident[:, :], in_=ident[:, :], compare_op=ALU.not_equal, fill=1.0,
                               base=0, pattern=[[-1, P]], channel_multiplier=1).then_inc(s_const, 1)
            pool.affine_select(out=earlier[:, :], in_=earlier[:, :], compare_op=ALU.is_gt, fill=0.0,
                               base=0, pattern=[[-1, EB]], channel_multiplier=1).then_inc(s_const, 1)
            pool.iota(thresholds[:, :], pattern=[[SUB, STRIPS - 1]], base=SUB, channel_multiplier=0,
                      allow_small_or_imprecise_dtypes=True).then_inc(s_const, 1)
            pool.iota(row_id[:, :], pattern=[[0, 1]], base=0, channel_multiplier=1,
                      allow_small_or_imprecise_dtypes=True).then_inc(s_const, 1)
            pool.memset(eps_t[:, :], EPS).then_inc(s_const, 1)
            pool.iota(bases[:, :], pattern=[[WIN * LANES, GATHERS]], base=0, channel_multiplier=WIN,
                      allow_small_or_imprecise_dtypes=True).then_inc(s_const, 1)
            pool.iota(iota_lo[:, :], pattern=[[1, P]], base=0, channel_multiplier=0,
                      allow_small_or_imprecise_dtypes=True).then_inc(s_const, 1)
            pool.iota(iota_key[:, :], pattern=[[1, KEYS]], base=0, channel_multiplier=0,
                      allow_small_or_imprecise_dtypes=True).then_inc(s_const, 1)
            pool.memset(ones[:, :], 1.0).then_inc(s_const, 1)
            pool.wait_ge(s_pv, PREP_CNT + 2)
            rows = by_window(prep(3, I32, GATHERS * EB), EB)
            for g in range(GATHERS):
                pool.indirect_dma_start(out=rows[:, g, :], out_offset=None, in_=dst.rearrange("(b e) -> b e", e=EB),
                                        in_offset=bass.IndirectOffsetOnAxis(ap=block_i[:, g:g + 1], axis=0))\
                    .then_inc(s_rows, 16)
            pool.wait_ge(s_pv, PREP_START)
            for i, arr, dt, s in ((1, dst, I32, s_wdst), (0, src, I32, s_wsrc), (2, edge_weight, F32, s_wwgt)):
                for g in range(GATHERS):
                    pool.indirect_dma_start(out=by_window(prep(i, dt))[:, g, :], out_offset=None,
                                            in_=arr.rearrange("(e o) -> e o", o=1),
                                            in_offset=bass.IndirectOffsetOnAxis(ap=start_i[:, g:g + 1], axis=0))\
                        .then_inc(s, 16)
            pool.wait_ge(s_flag, 1)
            fits = pool.value_load(flag[0:1, 0:1], min_val=0, max_val=1)
            with pool.If(fits):
                pool.wait_ge(s_colv, COL_BANKS)
                with pool.Fori(0, GATHERS) as t:
                    for k in range(BATCHES_PER_GATHER):
                        n = BATCHES_PER_GATHER * t + k
                        pool.wait_ge(s_hot, 2 * n + 2)
                        pool.sem_inc(s_mark_pool, 1)
                        weight = columns[:, 2, bass.ds(BATCH * n, BATCH)].rearrange("p (w o) -> p w o", o=1)
                        pool.tensor_tensor(hot_key[:, k % 2, :, 1, :], hot_key[:, k % 2, :, 0, :],
                                           weight.to_broadcast([P, BATCH, KEYS]), ALU.mult).then_inc(s_hotw, 1)
            with pool.Else():
                pool.wait_ge(s_zero, 16 * 2 * STRIPS)
                with pool.Fori(0, BLOCKS) as b:
                    pool.wait_ge(s_bv, START + BV * (b + 1))
                    pool.sem_inc(s_mark_pool, 1)
                    for adj, val, s in ((adj_w, w_sum, s_scw), (adj_c, count, s_scc)):
                        pool.indirect_dma_start(out=adj.rearrange("(e o) -> e o", o=1),
                                                out_offset=bass.IndirectOffsetOnAxis(ap=cell[:, 0:1], axis=0),
                                                in_=val[:, :], in_offset=None, compute_op=ALU.add).then_inc(s, 16)
                    pool.wait_ge(s_scw, 16 * (b + 1))
                    pool.wait_ge(s_scc, 16 * (b + 1))
                    pool.sem_inc(s_scattered, 1)

        @block.tensor
        def _(pe):
            pe.sem_inc(s_used, SLABS)
            pe.sem_inc(s_evac, FREE)
            pe.sem_inc(s_gate, FREE)
            for s in (s_gv, s_rz, s_n, s_ye, s_bv, s_scattered):
                pe.sem_inc(s, START)
            pe.sem_inc(s_bmm, AHEAD)
            pe.sem_inc(s_bev, 2 * AHEAD)
            pe.sem_inc(s_sfree, AHEAD)
            pe.wait_ge(s_const, N_CONST)
            pe.wait_ge(s_in, 16 * N_IN)
            for j, (c, n) in enumerate(CHUNKS):
                if j >= 2:
                    pe.wait_ge(s_setv, SET0 + j - 1)
                for k in range(n):
                    mm = pe.transpose(ps[:, 6 + j % 2, k * P:(k + 1) * P], Y[:, c + k, :], ident[:, :])
                mm.then_inc(s_setp, 1)
            for j in range(9):
                mm = pe.transpose(ps[:, j // 4, (j % 4) * P:(j % 4 + 1) * P], w_raw[:, j, :], ident[:, :])
            mm.then_inc(s_setp, 1)
            pe.wait_ge(s_setv, SET_ALL)

            def node_major(layer, w):
                for j, (c, n) in enumerate(CHUNKS):
                    pe.wait_ge(s_ye, START + NC * layer + max(j - 1, 0))
                    for k in range(n):
                        mm = pe.matmul(ps[:, 6 + j % 2, k * P:(k + 1) * P], xT[:, tile_cols(c + k)], w,
                                       start=True, stop=True)
                    mm.then_inc(s_yp, 1)
                pe.wait_ge(s_ye, START + NC * layer + NC)
                pe.sem_inc(s_mark_pe, 1)

            def aggregate(n, bank, last=True):
                pe.wait_ge(s_evac, n + 1)
                for s in range(SLABS):
                    pe.wait_ge(s_slab[s], 16 * (n + 1))
                    for k in range(SH):
                        h = s * SH + k
                        mm = pe.matmul(ps[:, bank, 0:GW], Y[:, h, :], ring[:, s, :, k, :],
                                       start=(h == 0), stop=(last and h == TILES - 1))
                    mm.then_inc(s_used, 1)

            def gates(n, par, g):
                xg = xT[:, bass.ds(g * GW, GW)]
                pe.wait_ge(s_evac, FREE + n + 1)
                pe.wait_ge(s_rz, START + 2 * n)
                pe.wait_ge(s_gv, START + GV * n)
                for bank, c in ((2, 0), (3, 1)):
                    pe.matmul(ps[:, bank, 0:GW], wT[:, c, :], aggS[par], start=True, stop=False)
                    pe.matmul(ps[:, bank, 0:GW], wT[:, 3 + c, :], xg, start=False, stop=True)
                pe.matmul(ps[:, 4, 0:GW], wT[:, 2, :], aggS[par], start=True, stop=True)
                pe.matmul(ps[:, 5, 0:GW], wT[:, 5, :], xg, start=True, stop=True).then_inc(s_gate, 1)

            pe.wait_ge(s_pv, PREP_COVER)
            pe.matmul(ps[0:1, 4, 0:1], covered[:, :], ones[:, :], start=True, stop=True).then_inc(s_cov, 1)
            pe.wait_ge(s_pv, PREP_ALL)
            pe.wait_ge(s_wwgt, 16 * GATHERS)
            pe.wait_ge(s_flag, 1)
            for j in range(COL_BANKS):
                kind, first = divmod(4 * j, GATHERS)
                values = by_window(prep((5, 1, 2)[kind]))
                if j >= 4:
                    pe.wait_ge(s_colv, j - 3)
                for k in range(4):
                    mm = pe.transpose(ps[:, j % 4, k * LANES:(k + 1) * LANES], values[:, first + k, :],
                                      ident[0:LANES, 0:LANES])
                mm.then_inc(s_colp, 1)
            fits = pe.value_load(flag[0:1, 0:1], min_val=0, max_val=1)
            with pe.If(fits):
                pe.wait_ge(s_colv, COL_BANKS)
                with pe.Fori(0, GATHERS) as t:
                    for k in range(BATCHES_PER_GATHER):
                        n = BATCHES_PER_GATHER * t + k
                        pe.wait_ge(s_hotw, n + 1)
                        pe.wait_ge(s_bev, 2 * (n + 1))
                        for w in range(BATCH):
                            place = ps[:, 4 * (k % 2) + w // 2, (w % 2) * 256:(w % 2) * 256 + 2 * KEYS]
                            mm = pe.matmul(place, hot_lo[:, k % 2, w, :],
                                           hot_key[:, k % 2, w, :, :].rearrange("p k x -> p (k x)"),
                                           start=True, stop=True)
                        mm.then_inc(s_bmm, 1)
            pe.wait_ge(s_built, 1)

            with pe.Fori(0, N_LAYERS) as l:
                n0 = l * GROUPS
                pe.wait_ge(s_gv, START + GV * n0)
                node_major(l, gw[:, bass.ds(l, 1), :].rearrange("p o f -> p (o f)"))
                aggregate(n0, 0)
                with pe.Fori(0, GROUPS // 2 - 1) as i:
                    n = n0 + 2 * i
                    aggregate(n + 1, 1)
                    gates(n, 0, 2 * i)
                    aggregate(n + 2, 0)
                    gates(n + 1, 1, 2 * i + 1)
                aggregate(n0 + GROUPS - 1, 1)
                gates(n0 + GROUPS - 2, 0, GROUPS - 2)
                gates(n0 + GROUPS - 1, 1, GROUPS - 1)

            def ln_forward(which):
                for j, (c, n) in enumerate(CHUNKS):
                    pe.wait_ge(s_lnv, which * LN_STEPS + NC + (LN_TAIL[j - 2] if j >= 2 else 0))
                    for k in range(n):
                        mm = pe.transpose(ps[:, 6 + j % 2, k * P:(k + 1) * P], xT[:, tile_cols(c + k)], ident[:, :])
                    mm.then_inc(s_lnp, 1)

            ln_forward(0)
            for j, (c, n) in enumerate(CHUNKS):
                pe.wait_ge(s_lnv, NC + LN_TAIL[j])
                if j >= 2:
                    pe.wait_ge(s_lnc, j - 1)
                    pe.wait_ge(s_lnd, j - 1)
                for k in range(n):
                    mm = pe.transpose(ps[:, 4 + j % 2, k * P:(k + 1) * P], Y[:, c + k, :], ident[:, :])
                mm.then_inc(s_lnb, 1)
            pe.wait_ge(s_lnc, NC)

            with pe.Fori(0, N_LAYERS) as l:
                n0 = (N_LAYERS + l) * GROUPS
                pe.wait_ge(s_evac, FREE + n0)
                pe.wait_ge(s_cur, 2 * (l + 1))
                node_major(N_LAYERS + l, wcur[:, :])
                with pe.Fori(0, GROUPS // 2) as i:
                    for par in range(2):
                        n = n0 + 2 * i + par
                        aggregate(n, par, last=False)
                        pe.matmul(ps[:, par, 0:GW], wcur[:, :], xT[:, bass.ds((2 * i + par) * GW, GW)],
                                  start=False, stop=True).then_inc(s_agg, 1)
            pe.wait_ge(s_evac, FREE + 2 * N_LAYERS * GROUPS)
            ln_forward(1)

        @block.scalar
        def _(act):
            for t, b in ((bih, b_ih), (bhh, b_hh)):
                for c in range(3):
                    act.dma_start(t[:, c:c + 1], b[c * P:(c + 1) * P].rearrange("(p o) -> p o", o=1))\
                       .then_inc(s_in, 16)
            for k, b in enumerate((b0, b1, b2)):
                act.dma_start(bg[:, k:k + 1], b.rearrange("(p o) -> p o", o=1)).then_inc(s_in, 16)

            def evac(n, par):
                act.wait_ge(s_used, SLABS * (n + 2))
                act.wait_ge(s_gate, n + 1)
                act.activation(aggS[par], ps[:, par, 0:GW], ACT.Copy).then_inc(s_evac, 1)

            def update(n):
                act.wait_ge(s_gate, FREE + n + 1)
                act.wait_ge(s_gv, START + GV * n)
                act.activation(r_t, ps[:, 2, 0:GW], ACT.Sigmoid, bias=brz[:, 0:1]).then_inc(s_rz, 1)
                act.activation(z_t, ps[:, 3, 0:GW], ACT.Sigmoid, bias=brz[:, 1:2]).then_inc(s_rz, 1)
                act.wait_ge(s_gv, START + GV * n + 2)
                act.activation(n_t, t_t, ACT.Tanh).then_inc(s_n, 1)

            act.wait_ge(s_flag, 1)
            fits = act.value_load(flag[0:1, 0:1], min_val=0, max_val=1)
            with act.If(fits):
                with act.Fori(0, GATHERS) as t:
                    for k in range(BATCHES_PER_GATHER):
                        n = BATCHES_PER_GATHER * t + k
                        b, part = divmod(k, STRIP_BATCHES)
                        if part == 0:
                            act.wait_ge(s_sfree, STRIPS_PER_GATHER * t + b + 1)
                        act.wait_ge(s_bmm, AHEAD + n + 1)
                        banks = ps[:, 4 * (k % 2):4 * (k % 2) + 4, :].rearrange("p b (w x) -> p (b w) x", w=2)
                        for kind in range(2):
                            cells = strip_buf[:, b, kind, :, part * BATCH * WIN:(part + 1) * BATCH * WIN]
                            act.activation(
                                cells.rearrange("p h (w d) -> p w d h", d=WIN),
                                banks[:, :, kind * KEYS:(kind + 1) * KEYS].rearrange("p w (d h) -> p w d h", d=WIN),
                                ACT.Copy).then_inc(s_bev, 1)

            act.wait_ge(s_setv, SET_ALL)
            with act.Fori(0, N_LAYERS) as l:
                n0 = l * GROUPS
                evac(n0, 0)
                with act.Fori(0, GROUPS // 2 - 1) as i:
                    n = n0 + 2 * i
                    evac(n + 1, 1)
                    update(n)
                    evac(n + 2, 0)
                    update(n + 1)
                evac(n0 + GROUPS - 1, 1)
                update(n0 + GROUPS - 2)
                update(n0 + GROUPS - 1)

            def ln_std(which):
                done = 0
                for j, (c, n) in enumerate(CHUNKS):
                    act.wait_ge(s_lnv, which * LN_STEPS + NC + (LN_TAIL[j - 1] if j else 0) + 2 * n)
                    act.activation(std[:, j % 2, 0:n], mv[:, j % 2, 0:n, 1:2].rearrange("p t o -> p (t o)"), ACT.Sqrt,
                                   bias=eps_t[:, 0:1]).then_inc(s_lna, 1)

            ln_std(0)
            for j, (c, n) in enumerate(CHUNKS):
                act.wait_ge(s_lnc, j + 1)
                act.activation(resT[:, tile_cols(c, n)], ps[:, 4 + j % 2, 0:n * P], ACT.Copy).then_inc(s_lnd, 1)
            with act.Fori(0, N_LAYERS) as l:
                act.wait_ge(s_cur, 2 * (l + 1))
                with act.Fori(0, GROUPS // 2) as i:
                    for par in range(2):
                        g = 2 * i + par
                        act.wait_ge(s_agg, l * GROUPS + g + 1)
                        act.activation(xT[:, bass.ds(g * GW, GW)], ps[:, par, 0:GW], ACT.Relu, bias=bcur[:, 0:1])\
                           .then_inc(s_evac, 1)
            ln_std(1)

        @block.vector
        def _(dve):
            dve.memset(Y[:, FULL, :], 0.0).then_inc(s_setv, 1)
            for j, (c, n) in enumerate(CHUNKS):
                dve.wait_ge(s_setp, j + 1)
                dve.tensor_copy(xT[:, tile_cols(c, n)], ps[:, 6 + j % 2, 0:n * P]).then_inc(s_setv, 1)
            dve.wait_ge(s_setp, NC + 1)
            for j in range(3):
                n = min(4, 9 - 4 * j)
                dve.tensor_copy(wT[:, 4 * j:4 * j + n, :], ps[:, j, 0:n * P].rearrange("p (c f) -> p c f", f=P))\
                   .then_inc(s_setv, 1)
            dve.tensor_tensor(brz[:, :], bih[:, 0:2], bhh[:, 0:2], ALU.add).then_inc(s_setv, 1)
            dve.wait_ge(s_const, N_CONST)
            prepared = [0]

            def prep_step(ins, wait=True):
                prepared[0] += 1
                ins.then_inc(s_pv, 1)
                if wait:
                    dve.wait_ge(s_pv, prepared[0])

            dve.wait_ge(s_first, 32)
            firsts_f = prep(5, F32, BLOCKS)
            prep_step(dve.tensor_copy(firsts_f, prep(4, I32, BLOCKS)))
            for g in range(GATHERS):
                prep_step(dve.tensor_scalar(prep(0, F32, BLOCKS), firsts_f, bases[:, g:g + 1], 0.0, ALU.is_lt, ALU.add,
                                            accum_out=n_blocks[:, g:g + 1]))
            prep_step(dve.tensor_scalar(n_blocks[:, :], n_blocks[:, :], -1.0, 0.0, ALU.add, ALU.max))
            prep_step(dve.tensor_copy(block_i[:, :], n_blocks[:, :]))
            dve.wait_ge(s_rows, 16 * GATHERS)
            rows = by_window(prep(3, I32, GATHERS * EB), EB)
            below = by_window(prep(5, F32, GATHERS * EB), EB)
            base_of = bases[:, :].rearrange("p (g o) -> p g o", o=1)
            prep_step(dve.tensor_tensor(below, rows, base_of.to_broadcast([LANES, GATHERS, EB]), ALU.is_lt))
            prep_step(dve.tensor_reduce(in_block[:, :], below, mybir.AxisListType.X, ALU.add))
            prep_step(dve.scalar_tensor_tensor(out=in_block[:, :], in0=n_blocks[:, :], scalar=float(EB),
                                               in1=in_block[:, :], op0=ALU.mult, op1=ALU.add))
            prep_step(dve.tensor_scalar(start_i[:, :], in_block[:, :], float(N_EDGES - SLOTS), None, ALU.min))
            assert prepared[0] == PREP_START
            dve.wait_ge(s_wdst, 16 * GATHERS)
            rel, inside = prep(3), prep(4)
            prep_step(dve.tensor_tensor(by_window(rel), by_window(prep(1, I32)),
                                        base_of.to_broadcast([LANES, GATHERS, SLOTS]), ALU.subtract))
            prep_step(dve.tensor_scalar(inside, rel, 0.0, None, ALU.is_ge))
            prep_step(dve.scalar_tensor_tensor(out=prep(5), in0=rel, scalar=float(WIN), in1=inside,
                                               op0=ALU.is_lt, op1=ALU.mult))
            prep_step(dve.tensor_tensor_reduce(inside, inside, prep(5), 1.0, 0.0, ALU.mult, ALU.add, covered[:, :]))
            assert prepared[0] == PREP_COVER
            dve.wait_ge(s_cov, 1)
            dve.tensor_scalar(flag[:, :], ps[0:1, 4, 0:1], float(N_EDGES), None, ALU.is_equal).then_inc(s_flag, 1)
            dve.wait_ge(s_wsrc, 16 * GATHERS)
            prep_step(dve.tensor_scalar(prep(4, I32), prep(0, I32), 7, None, ALU.logical_shift_right))
            prep_step(dve.scalar_tensor_tensor(out=prep(5), in0=rel, scalar=float(TILES), in1=prep(4, I32),
                                               op0=ALU.mult, op1=ALU.add))
            prep_step(dve.tensor_scalar(prep(4, I32), prep(0, I32), P - 1, None, ALU.bitwise_and))
            prep_step(dve.tensor_copy(prep(1), prep(4, I32)))
            assert prepared[0] == PREP_ALL
            for j in range(COL_BANKS):
                kind, first = divmod(4 * j, GATHERS)
                dve.wait_ge(s_colp, j + 1)
                dve.tensor_copy(columns[:, kind, first * LANES:(first + 4) * LANES], ps[:, j % 4, 0:4 * LANES])\
                   .then_inc(s_colv, 1)
            dve.wait_ge(s_colv, COL_BANKS)

            fits = dve.value_load(flag[0:1, 0:1], min_val=0, max_val=1)
            with dve.If(fits):
                with dve.Fori(0, GATHERS) as t:
                    for k in range(BATCHES_PER_GATHER):
                        n = BATCHES_PER_GATHER * t + k
                        dve.wait_ge(s_bmm, n + 1)

                        def column(kind, width):
                            c = columns[:, kind, bass.ds(BATCH * n, BATCH)].rearrange("p (w o) -> p w o", o=1)
                            return c.to_broadcast([P, BATCH, width])

                        dve.tensor_tensor(hot_key[:, k % 2, :, 0, :],
                                          iota_key[:, :].rearrange("p (o x) -> p o x", o=1).to_broadcast([P, BATCH, KEYS]),
                                          column(0, KEYS), ALU.is_equal).then_inc(s_hot, 1)
                        dve.tensor_tensor(hot_lo[:, k % 2, :, :],
                                          iota_lo[:, :].rearrange("p (o x) -> p o x", o=1).to_broadcast([P, BATCH, P]),
                                          column(1, P), ALU.is_equal).then_inc(s_hot, 1)
            with dve.Else():
                dve.memset(ring_flat[:, 0:ROW], 0.0).then_inc(s_zfill, 1)
                with dve.Fori(0, BLOCKS) as b:
                    for s in s_ld:
                        dve.wait_ge(s, 16 * (b + 1))
                    dve.wait_ge(s_scattered, START + b)
                    done = [0]

                    def step(ins):
                        done[0] += 1
                        ins.then_inc(s_bv, 1)
                        if done[0] < BV:
                            dve.wait_ge(s_bv, START + BV * b + done[0])

                    strip, major, minor, col, rep, keep, m1, m2 = (scal[:, i:i + 1] for i in range(8))
                    step(dve.tensor_scalar(same[:, :], src_r[:, :], src_c[:, 0:1], None, ALU.is_equal))
                    step(dve.scalar_tensor_tensor(out=both[:, :], in0=dst_r[:, :], scalar=dst_c[:, 0:1], in1=same[:, :],
                                                  op0=ALU.is_equal, op1=ALU.mult))
                    for other, acc in ((w_r, w_sum), (both, count), (earlier, n_before)):
                        step(dve.tensor_tensor_reduce(junk[:, :], both[:, :], other[:, :], 1.0, 0.0, ALU.mult, ALU.add,
                                                      acc[:, :]))
                    step(dve.tensor_scalar(lo_i[:, :], src_c[:, :], P - 1, None, ALU.bitwise_and))
                    step(dve.tensor_scalar(hi_i[:, :], src_c[:, :], 7, None, ALU.logical_shift_right))
                    step(dve.tensor_scalar(m1, dst_c[:, :], 1.0, None, ALU.mult))
                    step(dve.tensor_scalar(tjunk[:, :], thresholds[:, :], m1, 0.0, ALU.is_le, ALU.add,
                                           accum_out=strip))
                    step(dve.scalar_tensor_tensor(out=major, in0=strip, scalar=float(P), in1=lo_i[:, :],
                                                  op0=ALU.mult, op1=ALU.add))
                    step(dve.scalar_tensor_tensor(out=col, in0=strip, scalar=float(-SUB), in1=dst_c[:, :],
                                                  op0=ALU.mult, op1=ALU.add))
                    step(dve.scalar_tensor_tensor(out=minor, in0=hi_i[:, :], scalar=float(SUB), in1=col,
                                                  op0=ALU.mult, op1=ALU.add))
                    step(dve.tensor_scalar(rep, n_before[:, :], 0.0, None, ALU.is_gt))
                    step(dve.tensor_scalar(keep, n_before[:, :], 0.0, None, ALU.is_equal))
                    step(dve.tensor_scalar(m1, major, float(ROW), keep, ALU.mult, ALU.mult))
                    step(dve.scalar_tensor_tensor(out=part_i[:, 0:1], in0=rep, scalar=float(SIZE), in1=m1,
                                                  op0=ALU.mult, op1=ALU.add))
                    step(dve.tensor_scalar(m2, minor, keep, None, ALU.mult))
                    step(dve.scalar_tensor_tensor(out=part_i[:, 1:2], in0=rep, scalar=row_id[:, 0:1], in1=m2,
                                                  op0=ALU.mult, op1=ALU.add))
                    dve.sem_inc(s_mark_dve, 1)
                    step(dve.tensor_tensor(cell[:, :], part_i[:, 0:1], part_i[:, 1:2], ALU.add))
                    assert done[0] == BV
            dve.wait_ge(s_built, 1)
            dve.tensor_copy(resT, xT[:, :]).then_inc(s_setv, 1)
            dve.wait_ge(s_setv, SET_ALL + 1)

            def take_node_major(layer):
                for j, (c, n) in enumerate(CHUNKS):
                    dve.wait_ge(s_yp, NC * layer + j + 1)
                    dve.tensor_copy(Y[:, c:c + n, :], ps[:, 6 + j % 2, 0:n * P].rearrange("p (c f) -> p c f", f=P))\
                       .then_inc(s_ye, 1)

            with dve.Fori(0, N_LAYERS) as l:
                take_node_major(l)
                with dve.Fori(0, GROUPS) as g:
                    n = l * GROUPS + g
                    xg = xT[:, bass.ds(g * GW, GW)]
                    dve.wait_ge(s_gate, FREE + n + 1)
                    dve.wait_ge(s_n, START + n)
                    dve.wait_ge(s_rz, START + 2 * n + 1)
                    dve.scalar_tensor_tensor(out=t_t, in0=ps[:, 5, 0:GW], scalar=bhh[:, 2:3], in1=r_t,
                                             op0=ALU.add, op1=ALU.mult).then_inc(s_gv, 1)
                    dve.wait_ge(s_gv, START + GV * n + 1)
                    dve.scalar_tensor_tensor(out=t_t, in0=ps[:, 4, 0:GW], scalar=bih[:, 2:3], in1=t_t,
                                             op0=ALU.add, op1=ALU.add).then_inc(s_gv, 1)
                    dve.wait_ge(s_n, START + n + 1)
                    dve.tensor_tensor(xg, xg, n_t, ALU.subtract).then_inc(s_gv, 1)
                    dve.wait_ge(s_gv, START + GV * n + 3)
                    dve.wait_ge(s_rz, START + 2 * n + 2)
                    dve.tensor_tensor(xg, xg, z_t, ALU.mult).then_inc(s_gv, 1)
                    dve.wait_ge(s_gv, START + GV * n + 4)
                    dve.tensor_tensor(xg, xg, n_t, ALU.add).then_inc(s_gv, 1)

            def layer_norm(which):
                v0 = which * LN_STEPS
                for j, (c, n) in enumerate(CHUNKS):
                    dve.tensor_tensor(xT[:, tile_cols(c, n)], xT[:, tile_cols(c, n)], resT[:, tile_cols(c, n)],
                                      ALU.add).then_inc(s_lnv, 1)
                v = v0 + NC
                for j, (c, n) in enumerate(CHUNKS):
                    dve.wait_ge(s_lnp, which * NC + j + 1)
                    node = ps[:, 6 + j % 2, 0:n * P].rearrange("p (t f) -> p t f", f=P)
                    for k in range(n):
                        dve.bn_stats(stats[:, k, :], node[:, k, :]).then_inc(s_lnv, 1)
                    dve.wait_ge(s_lnv, v + n)
                    for k in range(n):
                        dve.bn_aggr(mv[:, j % 2, k, :], stats[:, k, :]).then_inc(s_lnv, 1)
                    dve.wait_ge(s_lna, which * NC + j + 1)
                    dve.reciprocal(rstd[:, j % 2, 0:n], std[:, j % 2, 0:n]).then_inc(s_lnv, 1)
                    dve.wait_ge(s_lnv, v + 2 * n + 1)
                    for k in range(n):
                        dve.tensor_scalar(Y[:, c + k, :], node[:, k, :], mv[:, j % 2, k, 0:1],
                                          rstd[:, j % 2, k:k + 1], ALU.subtract, ALU.mult).then_inc(s_lnv, 1)
                    v += 3 * n + 1

            dve.wait_ge(s_gv, START + GV * N_LAYERS * GROUPS)
            layer_norm(0)
            for j, (c, n) in enumerate(CHUNKS):
                dve.wait_ge(s_lnb, j + 1)
                dve.tensor_copy(xT[:, tile_cols(c, n)], ps[:, 4 + j % 2, 0:n * P]).then_inc(s_lnc, 1)
            with dve.Fori(0, N_LAYERS) as l:
                dve.wait_ge(s_evac, FREE + (N_LAYERS + l) * GROUPS)
                dve.tensor_copy(wcur[:, :], wT[:, bass.ds(6 + l, 1), :].rearrange("p o f -> p (o f)")).then_inc(s_cur, 1)
                dve.tensor_copy(bcur[:, :], bg[:, bass.ds(l, 1)]).then_inc(s_cur, 1)
                take_node_major(N_LAYERS + l)
            dve.wait_ge(s_evac, FREE + 2 * N_LAYERS * GROUPS)
            dve.wait_ge(s_lnd, NC)
            layer_norm(1)


_INS = ['x', 'src', 'dst', 'edge_weight', 'L0_gnn_weight', 'L0_gnn_w_ih', 'L0_gnn_w_hh', 'L0_gnn_b_ih', 'L0_gnn_b_hh',
        'L1_gnn_W0', 'L1_gnn_b0', 'L1_gnn_W1', 'L1_gnn_b1', 'L1_gnn_W2', 'L1_gnn_b2']


def kernel(**inputs):
    import numpy as _np
    import concourse.bacc as _bacc
    from concourse import mybir as _mybir
    from concourse.bass_utils import run_bass_kernel_spmd as _run

    nc = _bacc.Bacc("TRN2", target_bir_lowering=False, num_devices=1)
    arrays, args = {}, []
    for name in _INS:
        a = _np.ascontiguousarray(inputs[name])
        arrays[f"in_{name}"] = a
        args.append(nc.dram_tensor(f"in_{name}", a.shape, _mybir.dt.from_np(a.dtype), kind="ExternalInput").ap())
    args.append(nc.dram_tensor("out_0", (N_NODES, P), _mybir.dt.float32, kind="ExternalOutput").ap())
    gnn_program(nc, *args)
    r = _run(nc, [arrays], core_ids=[0])
    return r.results[0]["out_0"]
```

```python
from contextlib import ExitStack

import concourse.bass as bass
from concourse import mybir

F32 = mybir.dt.float32
I32 = mybir.dt.int32
I16 = mybir.dt.int16
F16 = mybir.dt.float16
BF16 = mybir.dt.bfloat16
ALU = mybir.AluOpType
ACT = mybir.ActivationFunctionType

P = 128
N_NODES = 6250
N_EDGES = 200000
N_LAYERS = 3
EPS = 1e-5
NORM_BOUND = 12.0
TINY = 2.0 ** -100
EXPONENT = 0x7F800000
MAGNITUDE = 0x7FFFFFFF
ONE_EXP = 1 << 23
BIAS = 127
HALF_TOP = 14
TILES = -(-N_NODES // P)
NODES = TILES * P
FULL = N_NODES // P
TAIL = N_NODES - FULL * P
GROUPS = 14
GW = NODES // GROUPS
SUB = GW // 4
PARTS = GW // SUB
STRIPS = NODES // SUB
SLABS = 7
SH = TILES // SLABS
ROW = TILES * SUB
SIZE = STRIPS * P * ROW
WIN = 2
SLOTS = P
SHARE = SLOTS // WIN
OWN = SHARE - 1
LANES = 112
GATHERS = NODES // WIN // LANES
WINDOWS = GATHERS * LANES
FOREIGN = P
PREPS = 4
PG = GATHERS // PREPS
BATCH = 8
BUFS = 4
PSUM_BUFS = 2
WPARTS = 3
STRIP_BATCHES = SUB // WIN // BATCH
STRIPS_PER_GATHER = WIN * LANES // SUB
BATCHES_PER_GATHER = STRIPS_PER_GATHER * STRIP_BATCHES
EB = 125
BLOCKS = N_EDGES // EB
CHUNK = 4
CHUNKS = [(c, min(CHUNK, TILES - c)) for c in range(0, TILES, CHUNK)]
NC = len(CHUNKS)


def gnn_program(nc, x, src, dst, firsts, edge_weight, gnn_w, w_ih, w_hh, b_ih, b_hh,
                W0, b0, W1, b1, W2, b2, out):
    ctx = ExitStack()
    with ctx:
        def sb(name, shape, dt=F32):
            return ctx.enter_context(nc.sbuf_tensor(name, shape, dt))

        def sem(name):
            return ctx.enter_context(nc.semaphore(name))

        adj_w = nc.dram_tensor("adj_w", [SIZE + P], F32).ap()
        adj_c = nc.dram_tensor("adj_c", [SIZE + P], F32).ap()
        adj_h = nc.dram_tensor("adj_h", [SIZE], F16).ap()

        def strip_rows(adj):
            return adj[0:SIZE].rearrange("(u p e) -> u p e", p=P, e=ROW)

        def strips(adj):
            return adj[0:SIZE].rearrange("(u p h c) -> p u h c", p=P, h=TILES, c=SUB)

        xT = sb("xT", [P, NODES])
        shared = sb("shared", [P, NODES + 6 * GW])
        KINDS = 2 + WIN
        transposed = shared[:, 0:KINDS * LANES].rearrange("p (k w) -> p k w", k=KINDS)
        columns = shared[:, KINDS * LANES:KINDS * LANES + (2 + WPARTS * WIN) * LANES].bitcast(BF16)\
            .rearrange("p (b k w) -> p b k w", b=2, k=2 + WPARTS * WIN)
        resT = shared[:, 0:NODES]

        def gate_buffer(i):
            return shared[:, NODES + i * GW:NODES + (i + 1) * GW]

        Y = sb("Y", [P, TILES, P])
        ring = sb("ring", [P, SLABS, PARTS, SH, SUB])
        ident = sb("ident", [P, P])
        aggS = [gate_buffer(0), gate_buffer(1)]
        r_t, z_t, t_t, n_t = (gate_buffer(i) for i in range(2, 6))
        w_raw = sb("w_raw", [P, 9, P])
        wT = sb("wT", [P, 9, P])
        gw = sb("gw", [P, N_LAYERS, P])
        wcur = sb("wcur", [P, P])
        bih = sb("bih", [P, 3])
        bhh = sb("bhh", [P, 3])
        brz = sb("brz", [P, 2])
        bg = sb("bg", [P, 3])
        bcur = sb("bcur", [P, 1])
        eps_t = sb("eps_t", [P, 1])
        averager = sb("averager", [P, P])
        row_averager = sb("row_averager", [P, GROUPS - 1 + P])
        w_abs = sb("w_abs", [P, P])
        w_row = sb("w_row", [P, P])
        x_tops = sb("x_tops", [P, GROUPS])
        x_top = sb("x_top", [P, 1])
        bound = sb("bound", [P, 1])
        expo = sb("expo", [P, 1], I32)
        scale = sb("scale", [P, 1], I32)
        unscale = sb("unscale", [P, 1], I32)
        bases = sb("bases", [LANES, GATHERS])
        n_blocks = sb("n_blocks", [LANES, GATHERS])
        in_block = sb("in_block", [LANES, GATHERS])
        block_i = sb("block_i", [LANES, GATHERS], I32)
        starts = sb("starts", [LANES, GATHERS])
        starts_i = sb("starts_i", [LANES, GATHERS], I32)
        below = sb("below", [LANES, WIN + 1, GATHERS])
        places = sb("places", [LANES, WIN, GATHERS])
        degrees = sb("degrees", [LANES, WIN, GATHERS])
        take = sb("take", [LANES, WIN, GATHERS + 2])
        take_i = sb("take_i", [LANES, WIN, GATHERS + 2], I32)
        take_now = sb("take_now", [LANES, WIN], I32)
        slot_lo = sb("slot_lo", [LANES, WIN, GATHERS + 1])
        slot_hi = sb("slot_hi", [LANES, WIN, GATHERS + 1])
        disorder = sb("disorder", [LANES, PREPS])
        covered = sb("covered", [LANES, 2])
        own_i = sb("own_i", [LANES, WIN, GATHERS], I32)
        own_tile = sb("own_tile", [LANES, WIN, GATHERS], I32)
        own_row = sb("own_row", [LANES, WIN, GATHERS], I32)
        own_key = sb("own_key", [LANES, WIN, GATHERS + 1])
        own_lo = sb("own_lo", [LANES, WIN, GATHERS + 1])
        slot_iota = sb("slot_iota", [LANES, SHARE])
        ones = sb("ones", [LANES, 1])
        flag = sb("flag", [1, 1], I32)
        iota_lo = sb("iota_lo", [P, P, BATCH], BF16)
        iota_key = sb("iota_key", [P, TILES, BATCH], BF16)
        src_c = sb("src_c", [EB, 1], I32)
        dst_c = sb("dst_c", [EB, 1], I32)
        src_r = sb("src_r", [EB, EB], I32)
        dst_r = sb("dst_r", [EB, EB], I32)
        w_r = sb("w_r", [EB, EB])
        same = sb("same", [EB, EB])
        both = sb("both", [EB, EB])
        junk = sb("junk", [EB, EB])
        earlier = sb("earlier", [EB, EB])
        thresholds = sb("thresholds", [EB, STRIPS - 1])
        tjunk = sb("tjunk", [EB, STRIPS - 1])
        row_id = sb("row_id", [EB, 1])
        w_sum = sb("w_sum", [EB, 1])
        count = sb("count", [EB, 1])
        n_before = sb("n_before", [EB, 1])
        lo_i = sb("lo_i", [EB, 1], I32)
        hi_i = sb("hi_i", [EB, 1], I32)
        scal = sb("scal", [EB, 8])
        part_i = sb("part_i", [EB, 2], I32)
        cell = sb("cell", [EB, 1], I32)
        ps = ctx.enter_context(nc.psum_tensor("ps", [P, 8, 512], F32))

        s_bases = sem("s_bases")
        s_const = sem("s_const")
        s_in = sem("s_in")
        s_zfill = sem("s_zfill")
        s_zero = sem("s_zero")
        s_ld = [sem(f"s_ld{i}") for i in range(5)]
        s_bv = sem("s_bv")
        s_scw = sem("s_scw")
        s_scc = sem("s_scc")
        s_scattered = sem("s_scattered")
        s_slab = [sem(f"s_slab{s}") for s in range(SLABS)]
        s_used = sem("s_used")
        s_setp = sem("s_setp")
        s_setv = sem("s_setv")
        s_yp = sem("s_yp")
        s_ye = sem("s_ye")
        s_agg = sem("s_agg")
        s_evac = sem("s_evac")
        s_gate = sem("s_gate")
        s_rz = sem("s_rz")
        s_gv = sem("s_gv")
        s_n = sem("s_n")
        s_cur = sem("s_cur")
        s_sum = sem("s_sum")
        s_mean = sem("s_mean")
        s_cent = sem("s_cent")
        s_sq = sem("s_sq")
        s_var = sem("s_var")
        s_std = sem("s_std")
        s_rec = sem("s_rec")
        s_spread = sem("s_spread")
        s_norm = sem("s_norm")
        s_res = sem("s_res")
        s_outp = sem("s_outp")
        s_outa = sem("s_outa")
        s_sc = sem("s_sc")
        s_bnd = sem("s_bnd")
        s_yh = sem("s_yh")
        s_mark = sem("s_mark")
        s_tops = sem("s_tops")
        s_out = sem("s_out")
        s_first = sem("s_first")
        s_pv = sem("s_pv")
        s_rows = [sem(f"s_rows{c}") for c in range(PREPS)]
        s_wdst = [sem(f"s_wdst{c}") for c in range(PREPS)]
        s_take = sem("s_take")
        s_wsrc = sem("s_wsrc")
        s_wwgt = sem("s_wwgt")
        s_own = sem("s_own")
        s_key = sem("s_key")
        s_cov = sem("s_cov")
        s_flag = sem("s_flag")
        s_colp = sem("s_colp")
        s_cola = sem("s_cola")
        s_colv = sem("s_colv")
        s_hot = sem("s_hot")
        s_zero_hot = sem("s_zero_hot")
        s_bmm = sem("s_bmm")
        s_bev = sem("s_bev")
        s_strip = [sem("s_strip0"), sem("s_strip1")]
        s_sfree = sem("s_sfree")
        s_mark_dve = sem("s_mark_dve")
        s_mark_pool = sem("s_mark_pool")
        s_mark_pe = sem("s_mark_pe")

        GV = 5
        BV = 19
        N_IN = 17
        N_CONST = 22
        AHEAD = 2
        KEY_STEPS = 7
        COL_STEPS = 2 * WPARTS
        KEYS_AT = 0
        TRANSPOSE_AT = 8
        BLOCK_STEPS, START_STEPS, DEGREE_STEPS = PG + 2, 4, 9
        order = [("block", 0)]
        for c in range(1, PREPS):
            order += [("block", c), ("start", c - 1)] + ([("degree", c - 2)] if c > 1 else [])
        order += [("start", PREPS - 1), ("degree", PREPS - 2), ("degree", PREPS - 1)]
        BLOCKS_READY, STARTS_READY, steps = {}, {}, 1
        for kind, c in order:
            steps += {"block": BLOCK_STEPS, "start": START_STEPS, "degree": DEGREE_STEPS}[kind]
            if kind != "degree":
                (BLOCKS_READY if kind == "block" else STARTS_READY)[c] = steps
        PREP_ALL = steps + 13
        START = 1
        FREE = 2
        SC = 9
        SET0 = 1
        SET_ALL = SET0 + NC + 3 + 1

        ring_flat = ring[:, :, :, :, :].rearrange("p s u h c -> p (s u h c)")

        def prep(i, dt=F32, width=GATHERS * SLOTS):
            v = ring_flat[0:LANES, i * GATHERS * SLOTS:i * GATHERS * SLOTS + width]
            return v if dt == F32 else v.bitcast(dt)

        def by_window(v, width=SLOTS):
            return v.rearrange("p (g e) -> p g e", e=width)

        strip_w = ring_flat[:, 0:2 * ROW].rearrange("p (b h c) -> p b h c", b=2, h=TILES)
        strip_h = ring_flat[:, 2 * ROW:3 * ROW].bitcast(F16).rearrange("p (b h c) -> p b h c", b=2, h=TILES)
        y_flat = Y[:, :, :].rearrange("p t f -> p (t f)")

        def buffer_of(par, k):
            return (par * BATCHES_PER_GATHER + k) % BUFS

        def hots(start, width):
            return y_flat[:, start:start + BUFS * BATCH * width // 2].bitcast(BF16)\
                .rearrange("p (b x w) -> p b x w", b=BUFS, w=BATCH)

        hot_lo = hots(0, P)
        after_lo = BUFS * BATCH * P // 2
        hot_key = hots(after_lo, TILES)
        after_key = after_lo + BUFS * BATCH * TILES // 2
        hot_weight = ring_flat[:, 3 * ROW:3 * ROW + BUFS * BATCH * WPARTS * WIN * TILES // 2].bitcast(BF16)\
            .rearrange("p (b x w) -> p b x w", b=BUFS, w=BATCH)

        def weigh(engine, par, k):
            buf, cols = buffer_of(par, k), WPARTS * WIN
            key = hot_key[:, buf, :, :].rearrange("p (o x) w -> p o x w", o=1)
            weight = columns[:, par, 2:2 + cols, k * BATCH:(k + 1) * BATCH].rearrange("p c (o w) -> p c o w", o=1)
            out = hot_weight[:, buf, :, :].rearrange("p (c x) w -> p c x w", x=TILES)
            return engine.tensor_tensor(out, key.to_broadcast([P, cols, TILES, BATCH]),
                                        weight.to_broadcast([P, cols, TILES, BATCH]), ALU.mult)

        def stage(i, dt=F32):
            v = y_flat[0:LANES, after_key + i * SLOTS:after_key + (i + 1) * SLOTS]
            return v if dt == F32 else v.bitcast(dt)

        src_now, key_now, lo_now, int_now, from_lo, to_hi = range(6)
        weights_now = (6, 7)
        COLUMN_BANK = 4 * ((TRANSPOSE_AT + 1) % PSUM_BUFS)

        ring_h = ring_flat[:, 0:SLABS * GW * SH // 2].bitcast(F16).rearrange(
            "p (s u h c) -> p s u h c", s=SLABS, u=PARTS, h=SH)
        Y_high = y_flat[:, 0:NODES // 2].bitcast(F16).rearrange("p (t f) -> p t f", f=P)
        Y_low = y_flat[:, NODES // 2:NODES].bitcast(F16).rearrange("p (t f) -> p t f", f=P)
        out_buf = ring_flat[:, 0:NODES].rearrange("p (t f) -> p t f", f=P)

        def group(t, g):
            return t[:, bass.ds(g * GW, GW)]

        def tile_cols(t, n=1):
            return slice(t * P, (t + n) * P)

        block = ctx.enter_context(nc.Block())

        @block.sync
        def _(sp):
            sp.dma_start(prep(4, I32, BLOCKS), firsts.rearrange("(o b) -> o b", o=1).to_broadcast([LANES, BLOCKS]))\
              .then_inc(s_first, 16)
            sp.wait_ge(s_setv, 1)
            sp.dma_start(Y[:, 0:FULL, :], x[0:FULL * P, :].rearrange("(t p) f -> p t f", p=P)).then_inc(s_in, 16)
            sp.dma_start(Y[0:TAIL, FULL, :], x[FULL * P:N_NODES, :]).then_inc(s_in, 16)
            sp.dma_start(w_raw[:, 0:3, :], w_ih.rearrange("(c p) f -> p c f", p=P)).then_inc(s_in, 16)
            sp.dma_start(w_raw[:, 3:6, :], w_hh.rearrange("(c p) f -> p c f", p=P)).then_inc(s_in, 16)
            for k, w in enumerate((W0, W1, W2)):
                sp.dma_start(w_raw[:, 6 + k, :], w).then_inc(s_in, 16)
            sp.dma_start(gw[:, :, :], gnn_w.rearrange("l i o -> i l o")).then_inc(s_in, 16)
            sp.wait_ge(s_flag, 1)
            fits = sp.value_load(flag[0:1, 0:1], min_val=0, max_val=1)
            with sp.If(fits):
                with sp.Fori(0, GATHERS) as t:
                    for b in range(STRIPS_PER_GATHER):
                        u = STRIPS_PER_GATHER * t + b
                        sp.wait_ge(s_bev, 2 * (PSUM_BUFS + STRIP_BATCHES * (u + 1)))
                        for adj, strip in ((adj_w, strip_w), (adj_h, strip_h)):
                            sp.dma_start(strip_rows(adj)[bass.ds(u, 1), :, :].rearrange("o p e -> (o p) e"),
                                         strip[:, b, :, :].rearrange("p h c -> p (h c)"))\
                              .then_inc(s_strip[b], 16)
                        sp.wait_ge(s_strip[b], 32 * (t + 1))
                        sp.sem_inc(s_sfree, 1)
            with sp.Else():
                sp.wait_ge(s_zfill, 1)
                for adj in (adj_w, adj_c):
                    for u in range(STRIPS):
                        sp.dma_start(adj[u * P * ROW:(u + 1) * P * ROW].rearrange("(p e) -> p e", p=P),
                                     ring_flat[:, 0:ROW]).then_inc(s_zero, 16)
                with sp.Fori(0, BLOCKS) as b:
                    edges = bass.ds(b * EB, EB)
                    sp.wait_ge(s_bv, START + BV * b)
                    cols = [(src_c, src), (dst_c, dst)]
                    for k, (t, a) in enumerate(cols):
                        sp.dma_start(t[:, :], a[edges].rearrange("(p o) -> p o", o=1)).then_inc(s_ld[k], 16)
                    for k, (t, a) in enumerate(((src_r, src), (dst_r, dst), (w_r, edge_weight))):
                        sp.dma_start(t[:, :], a[edges].rearrange("(o e) -> o e", o=1).to_broadcast([EB, EB]))\
                          .then_inc(s_ld[2 + k], 16)
                sp.wait_ge(s_scattered, START + BLOCKS)

            def stream(adj, dest, first):
                with sp.Fori(0, N_LAYERS) as l:
                    with sp.Fori(0, GROUPS) as g:
                        n = (first + l) * GROUPS + g
                        for s in range(SLABS):
                            sp.wait_ge(s_used, SLABS * n + s + 1)
                            sp.dma_start(dest[:, s, :, :, :],
                                         strips(adj)[:, bass.ds(PARTS * g, PARTS), s * SH:(s + 1) * SH, :])\
                              .then_inc(s_slab[s], 16)

            stream(adj_w, ring, 0)
            with sp.If(fits):
                stream(adj_h, ring_h, N_LAYERS)
            with sp.Else():
                stream(adj_c, ring, N_LAYERS)
            for j, (c, n) in enumerate(CHUNKS):
                sp.wait_ge(s_outa, j + 1)
                if c < FULL:
                    sp.dma_start(out[c * P:(c + n) * P, :].rearrange("(t p) f -> p t f", p=P), out_buf[:, c:c + n, :])\
                      .then_inc(s_out, 16)
                else:
                    sp.dma_start(out[FULL * P:N_NODES, :], out_buf[0:TAIL, FULL, :]).then_inc(s_out, 16)
            sp.wait_ge(s_out, 16 * NC)

        @block.gpsimd
        def _(pool):
            pool.iota(bases[:, :], pattern=[[WIN * LANES, GATHERS]], base=0, channel_multiplier=WIN,
                      allow_small_or_imprecise_dtypes=True).then_inc(s_bases, 1)
            pool.memset(ident[:, :], 0.0).then_inc(s_const, 1)
            pool.memset(earlier[:, :], 1.0).then_inc(s_const, 1)
            pool.wait_ge(s_const, 2)
            pool.affine_select(out=ident[:, :], in_=ident[:, :], compare_op=ALU.not_equal, fill=1.0,
                               base=0, pattern=[[-1, P]], channel_multiplier=1).then_inc(s_const, 1)
            pool.affine_select(out=earlier[:, :], in_=earlier[:, :], compare_op=ALU.is_gt, fill=0.0,
                               base=0, pattern=[[-1, EB]], channel_multiplier=1).then_inc(s_const, 1)
            pool.iota(thresholds[:, :], pattern=[[SUB, STRIPS - 1]], base=SUB, channel_multiplier=0,
                      allow_small_or_imprecise_dtypes=True).then_inc(s_const, 1)
            pool.iota(row_id[:, :], pattern=[[0, 1]], base=0, channel_multiplier=1,
                      allow_small_or_imprecise_dtypes=True).then_inc(s_const, 1)
            pool.memset(eps_t[:, :], EPS).then_inc(s_const, 1)
            pool.memset(averager[:, :], 1.0 / P).then_inc(s_const, 1)
            pool.memset(row_averager[:, 0:GROUPS - 1], 0.0).then_inc(s_const, 1)
            pool.memset(row_averager[:, GROUPS - 1:GROUPS], 1.0 / P).then_inc(s_const, 1)
            pool.memset(row_averager[:, GROUPS:GROUPS - 1 + P], 0.0).then_inc(s_const, 1)
            pool.memset(x_tops[:, :], NORM_BOUND).then_inc(s_const, 1)
            pool.iota(iota_lo[:, :, :], pattern=[[1, P], [0, BATCH]], base=0, channel_multiplier=0,
                      allow_small_or_imprecise_dtypes=True).then_inc(s_const, 1)
            pool.iota(iota_key[:, :, :], pattern=[[1, TILES], [0, BATCH]], base=-FOREIGN, channel_multiplier=0,
                      allow_small_or_imprecise_dtypes=True).then_inc(s_const, 1)
            pool.iota(slot_iota[:, :], pattern=[[1, SHARE]], base=0, channel_multiplier=0,
                      allow_small_or_imprecise_dtypes=True).then_inc(s_const, 1)
            pool.memset(ones[:, :], 1.0).then_inc(s_const, 1)
            pool.iota(own_i[:, :, :], pattern=[[1, WIN], [WIN * LANES, GATHERS]], base=0, channel_multiplier=WIN)\
                .then_inc(s_const, 1)
            pool.memset(own_key[:, :, GATHERS:GATHERS + 1], 0.0).then_inc(s_const, 1)
            pool.memset(own_lo[:, :, GATHERS:GATHERS + 1], 0.0).then_inc(s_const, 1)
            pool.memset(take[:, :, :], 0.0).then_inc(s_const, 1)
            pool.memset(slot_lo[:, :, :], 0.0).then_inc(s_const, 1)
            pool.memset(slot_hi[:, :, :], 0.0).then_inc(s_const, 1)
            rows = by_window(prep(3, I32, GATHERS * EB), EB)

            def gather_blocks(c):
                pool.wait_ge(s_pv, BLOCKS_READY[c])
                for g in range(c * PG, (c + 1) * PG):
                    pool.indirect_dma_start(out=rows[:, g, :], out_offset=None, in_=dst.rearrange("(b e) -> b e", e=EB),
                                            in_offset=bass.IndirectOffsetOnAxis(ap=block_i[:, g:g + 1], axis=0))\
                        .then_inc(s_rows[c], 16)

            def gather_destinations(c):
                pool.wait_ge(s_pv, STARTS_READY[c])
                for g in range(c * PG, (c + 1) * PG):
                    pool.indirect_dma_start(out=by_window(prep(1, I32))[:, g, :], out_offset=None,
                                            in_=dst.rearrange("(e o) -> e o", o=1),
                                            in_offset=bass.IndirectOffsetOnAxis(ap=starts_i[:, g:g + 1], axis=0))\
                        .then_inc(s_wdst[c], 16)

            gather_blocks(0)
            for c in range(1, PREPS):
                gather_blocks(c)
                gather_destinations(c - 1)
            gather_destinations(PREPS - 1)
            pool.wait_ge(s_flag, 1)
            fits = pool.value_load(flag[0:1, 0:1], min_val=0, max_val=1)
            with pool.If(fits):
                def add_own(t):
                    for to, own in ((key_now, own_key), (lo_now, own_lo)):
                        slots = stage(to).rearrange("p (d e) -> p d e", e=SHARE)[:, :, OWN:SHARE]
                        pool.tensor_copy(slots, own[:, :, bass.ds(t, 1)]).then_inc(s_own, 1)

                def gather(arr, dt, to, s):
                    for d in range(WIN):
                        pool.indirect_dma_start(out=stage(to[d], dt)[:, d * SHARE:d * SHARE + OWN], out_offset=None,
                                                in_=arr.rearrange("(e o) -> e o", o=1),
                                                in_offset=bass.IndirectOffsetOnAxis(ap=take_now[:, d:d + 1], axis=0))\
                            .then_inc(s, 16)

                def gather_sources(t):
                    pool.tensor_copy(take_now[:, :].rearrange("p (d o) -> p d o", o=1), take_i[:, :, bass.ds(t, 1)])\
                        .then_inc(s_take, 1)
                    pool.wait_ge(s_take, t + 1)
                    pool.sem_inc(s_mark_pool, 1)
                    gather(src, I32, (src_now, src_now), s_wsrc)

                def make_columns(t, par):
                    made = [0]

                    def col_step(ins):
                        made[0] += 1
                        ins.then_inc(s_colv, 1)
                        pool.wait_ge(s_colv, COL_STEPS * t + made[0])
                        pool.sem_inc(s_mark_pool, 1)

                    pool.wait_ge(s_cola, t + 1)
                    pool.sem_inc(s_mark_pool, 1)
                    rest = transposed[:, 2:KINDS, :]
                    col_step(pool.tensor_copy(columns[:, par, 0:2, :], transposed[:, 0:2, :]))
                    for p in range(WPARTS):
                        part = columns[:, par, 2 + p * WIN:2 + (p + 1) * WIN, :]
                        col_step(pool.tensor_copy(part, rest))
                        if p < WPARTS - 1:
                            col_step(pool.tensor_tensor(rest, rest, part, ALU.subtract))
                    assert made[0] == COL_STEPS

                pool.wait_ge(s_pv, PREP_ALL)
                pool.wait_ge(s_setp, NC)
                pool.memset(stage(src_now, I32), 0).then_inc(s_zero_hot, 1)
                pool.memset(stage(weights_now[0]), 0.0).then_inc(s_zero_hot, 1)
                pool.memset(stage(weights_now[1]), 0.0).then_inc(s_zero_hot, 1)
                pool.wait_ge(s_zero_hot, 3)
                gather_sources(0)
                gather(edge_weight, F32, weights_now, s_wwgt)
                pool.wait_ge(s_wwgt, 16 * WIN)
                pool.wait_ge(s_key, KEY_STEPS)
                add_own(0)
                gather_sources(1)
                pool.wait_ge(s_colp, 1)
                gather(edge_weight, F32, weights_now, s_wwgt)
                make_columns(0, 0)
                with pool.Fori(0, GATHERS // 2) as i:
                    for par in range(2):
                        t = 2 * i + par
                        pool.wait_ge(s_key, KEY_STEPS * (t + 2))
                        pool.sem_inc(s_mark_pool, 1)
                        add_own(t + 1)
                        pool.wait_ge(s_wwgt, 16 * WIN * (t + 2))
                        pool.sem_inc(s_mark_pool, 1)
                        gather_sources(t + 2)
                        pool.wait_ge(s_colp, t + 2)
                        pool.sem_inc(s_mark_pool, 1)
                        gather(edge_weight, F32, weights_now, s_wwgt)
                        make_columns(t + 1, 1 - par)
            with pool.Else():
                pool.wait_ge(s_zero, 16 * 2 * STRIPS)
                with pool.Fori(0, BLOCKS) as b:
                    pool.wait_ge(s_bv, START + BV * (b + 1))
                    pool.sem_inc(s_mark_pool, 1)
                    for adj, val, s in ((adj_w, w_sum, s_scw), (adj_c, count, s_scc)):
                        pool.indirect_dma_start(out=adj.rearrange("(e o) -> e o", o=1),
                                                out_offset=bass.IndirectOffsetOnAxis(ap=cell[:, 0:1], axis=0),
                                                in_=val[:, :], in_offset=None, compute_op=ALU.add).then_inc(s, 16)
                    pool.wait_ge(s_scw, 16 * (b + 1))
                    pool.wait_ge(s_scc, 16 * (b + 1))
                    pool.sem_inc(s_scattered, 1)

        @block.tensor
        def _(pe):
            pe.sem_inc(s_used, SLABS)
            pe.sem_inc(s_evac, FREE)
            pe.sem_inc(s_gate, FREE)
            for s in (s_gv, s_rz, s_n, s_ye, s_bv, s_scattered):
                pe.sem_inc(s, START)
            pe.sem_inc(s_bmm, BUFS)
            pe.sem_inc(s_bev, 2 * PSUM_BUFS)
            pe.sem_inc(s_sfree, AHEAD)
            pe.sem_inc(s_cent, AHEAD)
            pe.wait_ge(s_const, N_CONST)
            pe.wait_ge(s_in, 16 * N_IN)
            for j, (c, n) in enumerate(CHUNKS):
                if j >= 2:
                    pe.wait_ge(s_setv, SET0 + j - 1)
                for k in range(n):
                    mm = pe.transpose(ps[:, 6 + j % 2, k * P:(k + 1) * P], Y[:, c + k, :], ident[:, :])
                mm.then_inc(s_setp, 1)
            for j in range(9):
                mm = pe.transpose(ps[:, j // 4, (j % 4) * P:(j % 4 + 1) * P], w_raw[:, j, :], ident[:, :])
            mm.then_inc(s_setp, 1)

            def node_major(layer, w):
                for j, (c, n) in enumerate(CHUNKS):
                    pe.wait_ge(s_ye, START + NC * layer + max(j - 1, 0))
                    for k in range(n):
                        mm = pe.matmul(ps[:, 6 + j % 2, k * P:(k + 1) * P], xT[:, tile_cols(c + k)], w,
                                       start=True, stop=True)
                    mm.then_inc(s_yp, 1)
                pe.wait_ge(s_ye, START + NC * layer + NC)
                pe.sem_inc(s_mark_pe, 1)

            def aggregate(n, bank, last=True):
                pe.wait_ge(s_evac, n + 1)
                for s in range(SLABS):
                    pe.wait_ge(s_slab[s], 16 * (n + 1))
                    for k in range(SH):
                        h = s * SH + k
                        mm = pe.matmul(ps[:, bank, 0:GW], Y[:, h, :], ring[:, s, :, k, :],
                                       start=(h == 0), stop=(last and h == TILES - 1))
                    mm.then_inc(s_used, 1)

            def gates(n, par, g):
                xg = xT[:, bass.ds(g * GW, GW)]
                pe.wait_ge(s_evac, FREE + n + 1)
                pe.wait_ge(s_rz, START + 2 * n)
                pe.wait_ge(s_gv, START + GV * n)
                for bank, c in ((2, 0), (3, 1)):
                    pe.matmul(ps[:, bank, 0:GW], wT[:, c, :], aggS[par], start=True, stop=False)
                    pe.matmul(ps[:, bank, 0:GW], wT[:, 3 + c, :], xg, start=False, stop=True)
                pe.matmul(ps[:, 4, 0:GW], wT[:, 2, :], aggS[par], start=True, stop=True)
                pe.matmul(ps[:, 5, 0:GW], wT[:, 5, :], xg, start=True, stop=True).then_inc(s_gate, 1)

            pe.wait_ge(s_setv, SET_ALL - 1)
            pe.wait_ge(s_pv, PREP_ALL)
            for c in range(2):
                mm = pe.matmul(ps[0:1, 4, 0:1], covered[:, c:c + 1], ones[:, :], start=(c == 0), stop=(c == 1))
            mm.then_inc(s_cov, 1)
            pe.wait_ge(s_flag, 1)
            fits = pe.value_load(flag[0:1, 0:1], min_val=0, max_val=1)
            with pe.If(fits):
                def slots_to_partitions(t, bank):
                    pe.wait_ge(s_own, 2 * (t + 1))
                    pe.wait_ge(s_wwgt, 16 * WIN * (t + 1))
                    for kind, v in enumerate((key_now, lo_now) + weights_now):
                        mm = pe.transpose(ps[:, bank, kind * LANES:(kind + 1) * LANES], stage(v), ident[0:LANES, 0:LANES])
                    mm.then_inc(s_colp, 1)

                slots_to_partitions(0, COLUMN_BANK)
                pe.wait_ge(s_cola, 1)
                with pe.Fori(0, GATHERS // 2) as i:
                    for par in range(2):
                        t = 2 * i + par
                        for k in range(BATCHES_PER_GATHER):
                            n = BATCHES_PER_GATHER * t + k
                            bank, buf = 4 * (k % PSUM_BUFS), buffer_of(par, k)
                            pe.wait_ge(s_bev, 2 * (n + 1))
                            if k == TRANSPOSE_AT:
                                pe.wait_ge(s_bev, 2 * (n + 2))
                                slots_to_partitions(t + 1, COLUMN_BANK)
                            if k == TRANSPOSE_AT + 1:
                                pe.wait_ge(s_cola, t + 2)
                            pe.wait_ge(s_hot, 3 * n + 3)
                            for w in range(BATCH):
                                for d in range(WIN):
                                    slots = slice(d * SHARE, (d + 1) * SHARE)
                                    pe.matmul(ps[:, bank + d, w * TILES:(w + 1) * TILES], hot_lo[slots, buf, :, w],
                                              hot_key[slots, buf, :, w], start=True, stop=True)
                            for w in range(BATCH):
                                sums = ps[:, bank + WIN + w // 4, w % 4 * WIN * TILES:(w % 4 + 1) * WIN * TILES]
                                for part in range(WPARTS):
                                    cols = slice(part * WIN * TILES, (part + 1) * WIN * TILES)
                                    mm = pe.matmul(sums, hot_lo[:, buf, :, w], hot_weight[:, buf, cols, w],
                                                   start=(part == 0), stop=(part == WPARTS - 1))
                            mm.then_inc(s_bmm, 1)
                pe.wait_ge(s_bev, 2 * (PSUM_BUFS + BATCHES_PER_GATHER * GATHERS))
            pe.wait_ge(s_setv, SET_ALL)

            with pe.Fori(0, N_LAYERS) as l:
                n0 = l * GROUPS
                pe.wait_ge(s_gv, START + GV * n0)
                node_major(l, gw[:, bass.ds(l, 1), :].rearrange("p o f -> p (o f)"))
                aggregate(n0, 0)
                with pe.Fori(0, GROUPS // 2 - 1) as i:
                    n = n0 + 2 * i
                    aggregate(n + 1, 1)
                    gates(n, 0, 2 * i)
                    aggregate(n + 2, 0)
                    gates(n + 1, 1, 2 * i + 1)
                aggregate(n0 + GROUPS - 1, 1)
                gates(n0 + GROUPS - 2, 0, GROUPS - 2)
                gates(n0 + GROUPS - 1, 1, GROUPS - 1)

            def layer_norm(which):
                with pe.Fori(0, GROUPS // 2) as i:
                    for par in range(2):
                        g = 2 * i + par
                        n = which * GROUPS + g
                        pe.wait_ge(s_sum, n + 1)
                        pe.wait_ge(s_cent, n + 1)
                        pe.matmul(ps[:, par, 0:GW], averager[:, :], group(xT, g), start=True, stop=True)\
                          .then_inc(s_mean, 1)
                for g in range(GROUPS):
                    pe.wait_ge(s_sq, which * GROUPS + g + 1)
                    mm = pe.matmul(ps[:, 2, 0:GW], row_averager[:, GROUPS - 1 - g:GROUPS - 1 - g + P], group(y_flat, g),
                                   start=(g == 0), stop=(g == GROUPS - 1))
                mm.then_inc(s_var, 1)
                pe.wait_ge(s_rec, which + 1)
                for g in range(GROUPS):
                    if g >= 4:
                        pe.wait_ge(s_norm, which * GROUPS + g - 3)
                    pe.matmul(ps[:, g % 4, 0:GW], ident[:, g:g + 1].to_broadcast([P, P]), y_flat[:, 0:GW],
                              start=True, stop=True).then_inc(s_spread, 1)

            layer_norm(0)
            pe.wait_ge(s_norm, GROUPS)
            with pe.If(fits):
                with pe.Fori(0, N_LAYERS) as l:
                    layer = N_LAYERS + l
                    n0 = layer * GROUPS
                    pe.wait_ge(s_evac, FREE + n0)
                    pe.wait_ge(s_sc, SC * l + 2)
                    pe.matmul(ps[:, 2, 0:1], w_abs[:, :], x_top[:, :], start=True, stop=True).then_inc(s_bnd, 1)
                    pe.wait_ge(s_sc, SC * l + 7)
                    pe.transpose(ps[:, 3, 0:P], w_row[:, :], ident[:, :]).then_inc(s_bnd, 1)
                    pe.wait_ge(s_sc, SC * l + 9)
                    for j, (c, n) in enumerate(CHUNKS):
                        pe.wait_ge(s_ye, START + NC * layer + max(j - 3, 0))
                        for k in range(n):
                            mm = pe.matmul(ps[:, 4 + j % 4, k * P:(k + 1) * P], xT[:, tile_cols(c + k)], wcur[:, :],
                                           start=True, stop=True)
                        mm.then_inc(s_yp, 1)
                    pe.wait_ge(s_ye, START + NC * layer + NC)
                    pe.sem_inc(s_mark_pe, 1)
                    with pe.Fori(0, GROUPS // 2) as i:
                        for par in range(2):
                            n = n0 + 2 * i + par
                            pe.wait_ge(s_evac, n + 1)
                            for s in range(SLABS):
                                pe.wait_ge(s_slab[s], 16 * (n + 1))
                                for k in range(SH):
                                    for part in (Y_high, Y_low):
                                        mm = pe.matmul(ps[:, par, 0:GW], part[:, s * SH + k, :], ring_h[:, s, :, k, :],
                                                       start=(s == 0 and k == 0 and part is Y_high),
                                                       stop=(s == SLABS - 1 and k == SH - 1 and part is Y_low))
                                mm.then_inc(s_used, 1)
            with pe.Else():
                with pe.Fori(0, N_LAYERS) as l:
                    n0 = (N_LAYERS + l) * GROUPS
                    pe.wait_ge(s_evac, FREE + n0)
                    pe.wait_ge(s_cur, 2 * (l + 1))
                    node_major(N_LAYERS + l, wcur[:, :])
                    with pe.Fori(0, GROUPS // 2) as i:
                        for par in range(2):
                            n = n0 + 2 * i + par
                            aggregate(n, par, last=False)
                            pe.matmul(ps[:, par, 0:GW], wcur[:, :], xT[:, bass.ds((2 * i + par) * GW, GW)],
                                      start=False, stop=True).then_inc(s_agg, 1)
            pe.wait_ge(s_evac, FREE + 2 * N_LAYERS * GROUPS)
            layer_norm(1)
            for j, (c, n) in enumerate(CHUNKS):
                pe.wait_ge(s_norm, GROUPS + -(-(c + n) * P // GW))
                if j >= 4:
                    pe.wait_ge(s_outa, j - 3)
                for k in range(n):
                    mm = pe.transpose(ps[:, 4 + j % 4, k * P:(k + 1) * P], xT[:, tile_cols(c + k)], ident[:, :])
                mm.then_inc(s_outp, 1)

        @block.scalar
        def _(act):
            for t, b in ((bih, b_ih), (bhh, b_hh)):
                for c in range(3):
                    act.dma_start(t[:, c:c + 1], b[c * P:(c + 1) * P].rearrange("(p o) -> p o", o=1))\
                       .then_inc(s_in, 16)
            for k, b in enumerate((b0, b1, b2)):
                act.dma_start(bg[:, k:k + 1], b.rearrange("(p o) -> p o", o=1)).then_inc(s_in, 16)

            for j, (c, n) in enumerate(CHUNKS):
                act.wait_ge(s_setp, j + 1)
                act.activation(xT[:, tile_cols(c, n)], ps[:, 6 + j % 2, 0:n * P], ACT.Copy).then_inc(s_setv, 1)
            act.wait_ge(s_setp, NC + 1)
            for j in range(3):
                n = min(4, 9 - 4 * j)
                act.activation(wT[:, 4 * j:4 * j + n, :], ps[:, j, 0:n * P].rearrange("p (c f) -> p c f", f=P), ACT.Copy)\
                   .then_inc(s_setv, 1)

            def evac(n, par):
                act.wait_ge(s_used, SLABS * (n + 2))
                act.wait_ge(s_gate, n + 1)
                act.activation(aggS[par], ps[:, par, 0:GW], ACT.Copy).then_inc(s_evac, 1)

            def update(n):
                act.wait_ge(s_gate, FREE + n + 1)
                act.wait_ge(s_gv, START + GV * n)
                act.activation(r_t, ps[:, 2, 0:GW], ACT.Sigmoid, bias=brz[:, 0:1]).then_inc(s_rz, 1)
                act.activation(z_t, ps[:, 3, 0:GW], ACT.Sigmoid, bias=brz[:, 1:2]).then_inc(s_rz, 1)
                act.wait_ge(s_gv, START + GV * n + 2)
                act.activation(n_t, t_t, ACT.Tanh).then_inc(s_n, 1)

            act.wait_ge(s_flag, 1)
            fits = act.value_load(flag[0:1, 0:1], min_val=0, max_val=1)
            with act.If(fits):
                def take_columns(t):
                    act.wait_ge(s_colp, t + 1)
                    act.activation(transposed,
                                   ps[:, COLUMN_BANK, 0:KINDS * LANES].rearrange("p (k w) -> p k w", k=KINDS), ACT.Copy)\
                       .then_inc(s_cola, 1)

                take_columns(0)
                with act.Fori(0, GATHERS // 2) as i:
                    for par in range(2):
                        t = 2 * i + par
                        for k in range(BATCHES_PER_GATHER):
                            if k == TRANSPOSE_AT:
                                act.wait_ge(s_colv, COL_STEPS * (t + 1))
                                take_columns(t + 1)
                            n = BATCHES_PER_GATHER * t + k
                            b, part = divmod(k, STRIP_BATCHES)
                            if part == 0:
                                act.wait_ge(s_sfree, STRIPS_PER_GATHER * t + b + 1)
                            act.wait_ge(s_bmm, BUFS + n + 1)
                            bank = 4 * (k % PSUM_BUFS)
                            cols = slice(part * BATCH * WIN, (part + 1) * BATCH * WIN)
                            act.activation(strip_h[:, b, :, cols].rearrange("p h (w d) -> p d w h", d=WIN),
                                           ps[:, bank:bank + 2, 0:BATCH * TILES].rearrange("p d (w h) -> p d w h", h=TILES),
                                           ACT.Copy).then_inc(s_bev, 1)
                            act.activation(strip_w[:, b, :, cols].rearrange("p h (a c) -> p a c h", a=2),
                                           ps[:, bank + 2:bank + 4, 0:BATCH * TILES]
                                           .rearrange("p a (c h) -> p a c h", h=TILES),
                                           ACT.Copy).then_inc(s_bev, 1)

            act.wait_ge(s_setv, SET_ALL)
            with act.Fori(0, N_LAYERS) as l:
                n0 = l * GROUPS
                evac(n0, 0)
                with act.Fori(0, GROUPS // 2 - 1) as i:
                    n = n0 + 2 * i
                    evac(n + 1, 1)
                    update(n)
                    evac(n + 2, 0)
                    update(n + 1)
                evac(n0 + GROUPS - 1, 1)
                update(n0 + GROUPS - 2)
                update(n0 + GROUPS - 1)

            def layer_norm(which):
                with act.Fori(0, GROUPS) as g:
                    act.wait_ge(s_cent, AHEAD + which * GROUPS + g + 1)
                    act.activation(group(y_flat, g), group(xT, g), ACT.Square).then_inc(s_sq, 1)
                act.wait_ge(s_var, which + 1)
                act.activation(y_flat[:, 0:GW], ps[:, 2, 0:GW], ACT.Sqrt, bias=eps_t[:, 0:1]).then_inc(s_std, 1)

            layer_norm(0)
            with act.Fori(0, GROUPS) as g:
                act.wait_ge(s_norm, g + 1)
                act.activation(group(resT, g), group(xT, g), ACT.Copy).then_inc(s_res, 1)
            act.wait_ge(s_res, GROUPS)
            with act.If(fits):
                with act.Fori(0, N_LAYERS) as l:
                    for j, (c, n) in enumerate(CHUNKS):
                        act.wait_ge(s_yp, NC * (N_LAYERS + l) + j + 1)
                        act.activation(Y_high[:, c:c + n, :],
                                       ps[:, 4 + j % 4, 0:n * P].rearrange("p (t f) -> p t f", f=P), ACT.Copy)\
                           .then_inc(s_yh, 1)
                    with act.Fori(0, GROUPS // 2) as i:
                        for par in range(2):
                            g = 2 * i + par
                            act.wait_ge(s_used, SLABS * ((N_LAYERS + l) * GROUPS + g + 2))
                            act.activation(group(xT, g), ps[:, par, 0:GW], ACT.Relu, bias=bcur[:, 0:1],
                                           scale=unscale[:, 0:1].bitcast(F32)).then_inc(s_evac, 1)
            with act.Else():
                with act.Fori(0, N_LAYERS) as l:
                    act.wait_ge(s_cur, 2 * (l + 1))
                    with act.Fori(0, GROUPS // 2) as i:
                        for par in range(2):
                            g = 2 * i + par
                            act.wait_ge(s_agg, l * GROUPS + g + 1)
                            act.activation(xT[:, bass.ds(g * GW, GW)], ps[:, par, 0:GW], ACT.Relu, bias=bcur[:, 0:1])\
                               .then_inc(s_evac, 1)
            layer_norm(1)
            for j, (c, n) in enumerate(CHUNKS):
                act.wait_ge(s_outp, j + 1)
                act.activation(out_buf[:, c:c + n, :],
                               ps[:, 4 + j % 4, 0:n * P].rearrange("p (t f) -> p t f", f=P), ACT.Copy)\
                   .then_inc(s_outa, 1)

        @block.vector
        def _(dve):
            dve.memset(Y[:, FULL, :], 0.0).then_inc(s_setv, 1)
            dve.wait_ge(s_bases, 1)
            prepared = [0]

            def prep_step(ins):
                prepared[0] += 1
                ins.then_inc(s_pv, 1)
                dve.wait_ge(s_pv, prepared[0])

            dve.wait_ge(s_first, 16)
            firsts_s = prep(5, I16, 2 * BLOCKS)[:, 0:BLOCKS]
            prep_step(dve.tensor_copy(firsts_s, prep(4, I32, BLOCKS)))
            rows = by_window(prep(3, I32, GATHERS * EB), EB)

            def base_of(part, width):
                return bases[:, part].rearrange("p (g o) -> p g o", o=1).to_broadcast([LANES, PG, width])

            def prepare_block(c, part):
                for g in range(c * PG, (c + 1) * PG):
                    prep_step(dve.tensor_scalar(prep(0, BF16, BLOCKS)[:, 0:BLOCKS], firsts_s, bases[:, g:g + 1], 0.0,
                                                ALU.is_lt, ALU.add, accum_out=n_blocks[:, g:g + 1]))
                prep_step(dve.tensor_scalar(n_blocks[:, part], n_blocks[:, part], -1.0, 0.0, ALU.add, ALU.max))
                prep_step(dve.tensor_copy(block_i[:, part], n_blocks[:, part]))

            def prepare_start(c, part):
                dve.wait_ge(s_rows[c], 16 * PG)
                less = by_window(prep(4, F32, PG * EB), EB)
                prep_step(dve.tensor_tensor(less, rows[:, part, :], base_of(part, EB), ALU.is_lt))
                prep_step(dve.tensor_reduce(in_block[:, part], less, mybir.AxisListType.X, ALU.add))
                prep_step(dve.scalar_tensor_tensor(out=starts[:, part], in0=n_blocks[:, part], scalar=float(EB),
                                                   in1=in_block[:, part], op0=ALU.mult, op1=ALU.add))
                prep_step(dve.tensor_scalar(starts_i[:, part], starts[:, part], float(N_EDGES - SLOTS), None, ALU.min))

            def prepare_degree(c, part):
                dve.wait_ge(s_wdst[c], 16 * PG)
                rel, less = by_window(prep(2, F32, PG * SLOTS)), by_window(prep(4, F32, PG * SLOTS))
                prep_step(dve.tensor_tensor(rel, by_window(prep(1, I32))[:, part, :], base_of(part, SLOTS),
                                            ALU.subtract))
                for d in range(WIN + 1):
                    prep_step(dve.tensor_scalar(less, rel, float(d), None, ALU.is_lt))
                    prep_step(dve.tensor_reduce(below[:, d, part], less, mybir.AxisListType.X, ALU.add))
                falls = less[:, :, 0:SLOTS - 1]
                prep_step(dve.tensor_tensor(falls, rel[:, :, 0:SLOTS - 1], rel[:, :, 1:SLOTS], ALU.is_gt))
                prep_step(dve.tensor_scalar(falls, falls, 1.0, 0.0, ALU.mult, ALU.add, accum_out=disorder[:, c:c + 1]))

            for kind, c in order:
                part = slice(c * PG, (c + 1) * PG)
                {"block": prepare_block, "start": prepare_start, "degree": prepare_degree}[kind](c, part)
            dve.wait_ge(s_const, N_CONST)
            real = slice(0, GATHERS)
            prep_step(dve.tensor_scalar(starts[:, :], starts[:, :], float(N_EDGES - SLOTS), None, ALU.min))
            prep_step(dve.tensor_tensor(places[:, :, :], below[:, 0:WIN, :],
                                        starts[:, :].rearrange("p (o g) -> p o g", o=1)
                                        .to_broadcast([LANES, WIN, GATHERS]), ALU.add))
            prep_step(dve.tensor_tensor(degrees[:, :, :], below[:, 1:WIN + 1, :], below[:, 0:WIN, :], ALU.subtract))
            prep_step(dve.tensor_scalar(take[:, :, real], places[:, :, :], float(N_EDGES - OWN), None, ALU.min))
            prep_step(dve.tensor_copy(take_i[:, :, :], take[:, :, :]))
            prep_step(dve.tensor_tensor(slot_lo[:, :, real], places[:, :, :], take[:, :, real], ALU.subtract))
            prep_step(dve.tensor_tensor(slot_hi[:, :, real], slot_lo[:, :, real], degrees[:, :, :], ALU.add))
            prep_step(dve.tensor_scalar(degrees[:, :, :], degrees[:, :, :], float(OWN), 0.0, ALU.min, ALU.add,
                                        accum_out=covered[:, 0:1]))
            prep_step(dve.tensor_scalar(disorder[:, :], disorder[:, :], float(-1), 0.0, ALU.mult, ALU.add,
                                        accum_out=covered[:, 1:2]))
            prep_step(dve.tensor_scalar(own_tile[:, :, :], own_i[:, :, :], 7, None, ALU.logical_shift_right))
            prep_step(dve.tensor_scalar(own_row[:, :, :], own_i[:, :, :], P - 1, None, ALU.bitwise_and))
            prep_step(dve.tensor_scalar(own_key[:, :, real], own_tile[:, :, :], float(-FOREIGN), None, ALU.add))
            prep_step(dve.tensor_copy(own_lo[:, :, real], own_row[:, :, :]))
            assert prepared[0] == PREP_ALL
            dve.wait_ge(s_cov, 1)
            dve.tensor_scalar(flag[:, :], ps[0:1, 4, 0:1], float(N_EDGES), None, ALU.is_equal).then_inc(s_flag, 1)
            dve.wait_ge(s_flag, 1)

            dve.wait_ge(s_setp, NC + 1)
            dve.tensor_tensor(brz[:, :], bih[:, 0:2], bhh[:, 0:2], ALU.add).then_inc(s_setv, 1)
            fits = dve.value_load(flag[0:1, 0:1], min_val=0, max_val=1)
            with dve.If(fits):
                def by_share(v):
                    return v.rearrange("p (d e) -> p d e", e=SHARE)

                def make_keys(t):
                    made = [0]

                    def key_step(ins):
                        made[0] += 1
                        ins.then_inc(s_key, 1)
                        dve.wait_ge(s_key, KEY_STEPS * t + made[0])

                    def edge_of(bounds):
                        return bounds[:, :, bass.ds(t, 1)].to_broadcast([LANES, WIN, SHARE])

                    slot = slot_iota[:, :].rearrange("p (o e) -> p o e", o=1).to_broadcast([LANES, WIN, SHARE])
                    key_step(dve.tensor_tensor(by_share(stage(from_lo)), slot, edge_of(slot_lo), ALU.is_ge))
                    key_step(dve.tensor_tensor(by_share(stage(to_hi)), slot, edge_of(slot_hi), ALU.is_lt))
                    key_step(dve.tensor_tensor(stage(to_hi), stage(to_hi), stage(from_lo), ALU.mult))
                    dve.wait_ge(s_wsrc, 16 * WIN * (t + 1))
                    key_step(dve.tensor_scalar(stage(int_now, I32), stage(src_now, I32), 7, None,
                                               ALU.logical_shift_right))
                    key_step(dve.scalar_tensor_tensor(out=stage(key_now), in0=stage(to_hi), scalar=float(-FOREIGN),
                                                      in1=stage(int_now, I32), op0=ALU.mult, op1=ALU.add))
                    key_step(dve.tensor_scalar(stage(int_now, I32), stage(src_now, I32), P - 1, None, ALU.bitwise_and))
                    key_step(dve.tensor_copy(stage(lo_now), stage(int_now, I32)))
                    assert made[0] == KEY_STEPS

                make_keys(0)
                with dve.Fori(0, GATHERS // 2) as i:
                    for par in range(2):
                        t = 2 * i + par
                        dve.wait_ge(s_colv, COL_STEPS * (t + 1))
                        for k in range(BATCHES_PER_GATHER):
                            if k == KEYS_AT:
                                dve.wait_ge(s_colp, t + 1)
                                make_keys(t + 1)
                            n = BATCHES_PER_GATHER * t + k
                            dve.wait_ge(s_bmm, n + 1)
                            for hot, iota, kind in ((hot_key, iota_key, 0), (hot_lo, iota_lo, 1)):
                                values = columns[:, par, kind, k * BATCH:(k + 1) * BATCH]\
                                    .rearrange("p (o w) -> p o w", o=1).to_broadcast(list(iota.shape))
                                dve.tensor_tensor(hot[:, buffer_of(par, k), :, :], iota[:, :, :], values, ALU.is_equal)\
                                   .then_inc(s_hot, 1)
                            dve.wait_ge(s_hot, 3 * n + 1)
                            weigh(dve, par, k).then_inc(s_hot, 1)
                dve.wait_ge(s_wsrc, 16 * WIN * (GATHERS + 2))
                dve.wait_ge(s_wwgt, 16 * WIN * (GATHERS + 2))
                dve.wait_ge(s_colv, COL_STEPS * (GATHERS + 1))
                dve.wait_ge(s_hot, 3 * BATCHES_PER_GATHER * GATHERS)
            with dve.Else():
                dve.memset(ring_flat[:, 0:ROW], 0.0).then_inc(s_zfill, 1)
                with dve.Fori(0, BLOCKS) as b:
                    for s in s_ld:
                        dve.wait_ge(s, 16 * (b + 1))
                    dve.wait_ge(s_scattered, START + b)
                    done = [0]

                    def step(ins):
                        done[0] += 1
                        ins.then_inc(s_bv, 1)
                        if done[0] < BV:
                            dve.wait_ge(s_bv, START + BV * b + done[0])

                    strip, major, minor, col, rep, keep, m1, m2 = (scal[:, i:i + 1] for i in range(8))
                    step(dve.tensor_scalar(same[:, :], src_r[:, :], src_c[:, 0:1], None, ALU.is_equal))
                    step(dve.scalar_tensor_tensor(out=both[:, :], in0=dst_r[:, :], scalar=dst_c[:, 0:1], in1=same[:, :],
                                                  op0=ALU.is_equal, op1=ALU.mult))
                    for other, acc in ((w_r, w_sum), (both, count), (earlier, n_before)):
                        step(dve.tensor_tensor_reduce(junk[:, :], both[:, :], other[:, :], 1.0, 0.0, ALU.mult, ALU.add,
                                                      acc[:, :]))
                    step(dve.tensor_scalar(lo_i[:, :], src_c[:, :], P - 1, None, ALU.bitwise_and))
                    step(dve.tensor_scalar(hi_i[:, :], src_c[:, :], 7, None, ALU.logical_shift_right))
                    step(dve.tensor_scalar(m1, dst_c[:, :], 1.0, None, ALU.mult))
                    step(dve.tensor_scalar(tjunk[:, :], thresholds[:, :], m1, 0.0, ALU.is_le, ALU.add,
                                           accum_out=strip))
                    step(dve.scalar_tensor_tensor(out=major, in0=strip, scalar=float(P), in1=lo_i[:, :],
                                                  op0=ALU.mult, op1=ALU.add))
                    step(dve.scalar_tensor_tensor(out=col, in0=strip, scalar=float(-SUB), in1=dst_c[:, :],
                                                  op0=ALU.mult, op1=ALU.add))
                    step(dve.scalar_tensor_tensor(out=minor, in0=hi_i[:, :], scalar=float(SUB), in1=col,
                                                  op0=ALU.mult, op1=ALU.add))
                    step(dve.tensor_scalar(rep, n_before[:, :], 0.0, None, ALU.is_gt))
                    step(dve.tensor_scalar(keep, n_before[:, :], 0.0, None, ALU.is_equal))
                    step(dve.tensor_scalar(m1, major, float(ROW), keep, ALU.mult, ALU.mult))
                    step(dve.scalar_tensor_tensor(out=part_i[:, 0:1], in0=rep, scalar=float(SIZE), in1=m1,
                                                  op0=ALU.mult, op1=ALU.add))
                    step(dve.tensor_scalar(m2, minor, keep, None, ALU.mult))
                    step(dve.scalar_tensor_tensor(out=part_i[:, 1:2], in0=rep, scalar=row_id[:, 0:1], in1=m2,
                                                  op0=ALU.mult, op1=ALU.add))
                    dve.sem_inc(s_mark_dve, 1)
                    step(dve.tensor_tensor(cell[:, :], part_i[:, 0:1], part_i[:, 1:2], ALU.add))
                    assert done[0] == BV
            dve.wait_ge(s_setv, SET_ALL)
            dve.tensor_copy(resT, xT[:, :]).then_inc(s_setv, 1)
            dve.wait_ge(s_setv, SET_ALL + 1)

            def take_node_major(layer):
                for j, (c, n) in enumerate(CHUNKS):
                    dve.wait_ge(s_yp, NC * layer + j + 1)
                    dve.tensor_copy(Y[:, c:c + n, :], ps[:, 6 + j % 2, 0:n * P].rearrange("p (c f) -> p c f", f=P))\
                       .then_inc(s_ye, 1)

            with dve.Fori(0, N_LAYERS) as l:
                take_node_major(l)
                with dve.Fori(0, GROUPS) as g:
                    n = l * GROUPS + g
                    xg = xT[:, bass.ds(g * GW, GW)]
                    dve.wait_ge(s_gate, FREE + n + 1)
                    dve.wait_ge(s_n, START + n)
                    dve.wait_ge(s_rz, START + 2 * n + 1)
                    dve.scalar_tensor_tensor(out=t_t, in0=ps[:, 5, 0:GW], scalar=bhh[:, 2:3], in1=r_t,
                                             op0=ALU.add, op1=ALU.mult).then_inc(s_gv, 1)
                    dve.wait_ge(s_gv, START + GV * n + 1)
                    dve.scalar_tensor_tensor(out=t_t, in0=ps[:, 4, 0:GW], scalar=bih[:, 2:3], in1=t_t,
                                             op0=ALU.add, op1=ALU.add).then_inc(s_gv, 1)
                    dve.wait_ge(s_n, START + n + 1)
                    dve.tensor_tensor(xg, xg, n_t, ALU.subtract).then_inc(s_gv, 1)
                    dve.wait_ge(s_gv, START + GV * n + 3)
                    dve.wait_ge(s_rz, START + 2 * n + 2)
                    dve.tensor_tensor(xg, xg, z_t, ALU.mult).then_inc(s_gv, 1)
                    dve.wait_ge(s_gv, START + GV * n + 4)
                    dve.tensor_tensor(xg, xg, n_t, ALU.add).then_inc(s_gv, 1)

            def layer_norm(which):
                with dve.Fori(0, GROUPS) as g:
                    dve.tensor_tensor(group(xT, g), group(xT, g), group(resT, g), ALU.add).then_inc(s_sum, 1)
                with dve.Fori(0, GROUPS // 2) as i:
                    for par in range(2):
                        g = 2 * i + par
                        dve.wait_ge(s_mean, which * GROUPS + g + 1)
                        dve.tensor_tensor(group(xT, g), group(xT, g), ps[:, par, 0:GW], ALU.subtract)\
                           .then_inc(s_cent, 1)
                dve.wait_ge(s_std, which + 1)
                dve.reciprocal(y_flat[:, 0:GW], y_flat[:, 0:GW]).then_inc(s_rec, 1)
                for g in range(GROUPS):
                    dve.wait_ge(s_spread, which * GROUPS + g + 1)
                    dve.tensor_tensor(group(xT, g), group(xT, g), ps[:, g % 4, 0:GW], ALU.mult).then_inc(s_norm, 1)

            dve.wait_ge(s_gv, START + GV * N_LAYERS * GROUPS)
            layer_norm(0)
            with dve.If(fits):
                with dve.Fori(0, N_LAYERS) as l:
                    layer = N_LAYERS + l
                    dve.wait_ge(s_evac, FREE + layer * GROUPS)
                    scaled = [0]

                    def sc_step(ins, wait=True):
                        scaled[0] += 1
                        ins.then_inc(s_sc, 1)
                        if wait:
                            dve.wait_ge(s_sc, SC * l + scaled[0])

                    def one(t):
                        return t[:, bass.ds(2 * N_LAYERS + l, 1), :].rearrange("p o f -> p (o f)")

                    sc_step(dve.tensor_scalar(w_abs[:, :].bitcast(I32), one(wT).bitcast(I32), MAGNITUDE, None,
                                              ALU.bitwise_and))
                    sc_step(dve.tensor_reduce(x_top[:, :], x_tops[:, :], mybir.AxisListType.X, ALU.max))
                    dve.wait_ge(s_bnd, 2 * l + 1)
                    sc_step(dve.tensor_scalar(bound[:, :], ps[:, 2, 0:1], TINY, None, ALU.max))
                    sc_step(dve.tensor_scalar(expo[:, :], bound[:, :].bitcast(I32), EXPONENT, None, ALU.bitwise_and))
                    sc_step(dve.tensor_scalar(scale[:, :], expo[:, :], -1.0, float((2 * BIAS + HALF_TOP) * ONE_EXP),
                                              ALU.mult, ALU.add))
                    sc_step(dve.tensor_scalar(unscale[:, :], expo[:, :], float(-HALF_TOP * ONE_EXP), None, ALU.add))
                    sc_step(dve.tensor_scalar(w_row[:, :], one(w_raw), scale[:, 0:1].bitcast(F32), None, ALU.mult))
                    dve.wait_ge(s_bnd, 2 * l + 2)
                    sc_step(dve.tensor_copy(wcur[:, :], ps[:, 3, 0:P]))
                    sc_step(dve.tensor_copy(bcur[:, :], bg[:, bass.ds(l, 1)]), wait=False)
                    assert scaled[0] == SC
                    for j, (c, n) in enumerate(CHUNKS):
                        dve.wait_ge(s_yh, NC * l + j + 1)
                        dve.tensor_tensor(Y_low[:, c:c + n, :],
                                          ps[:, 4 + j % 4, 0:n * P].rearrange("p (t f) -> p t f", f=P),
                                          Y_high[:, c:c + n, :], ALU.subtract).then_inc(s_ye, 1)
                    with dve.Fori(0, GROUPS) as g:
                        dve.wait_ge(s_evac, FREE + layer * GROUPS + g + 1)
                        dve.sem_inc(s_mark, 1)
                        dve.tensor_reduce(x_tops[:, bass.ds(g, 1)], group(xT, g), mybir.AxisListType.X, ALU.max)\
                           .then_inc(s_tops, 1)
                    dve.wait_ge(s_tops, (l + 1) * GROUPS)
            with dve.Else():
                with dve.Fori(0, N_LAYERS) as l:
                    dve.wait_ge(s_evac, FREE + (N_LAYERS + l) * GROUPS)
                    dve.tensor_copy(wcur[:, :], wT[:, bass.ds(6 + l, 1), :].rearrange("p o f -> p (o f)")).then_inc(s_cur, 1)
                    dve.tensor_copy(bcur[:, :], bg[:, bass.ds(l, 1)]).then_inc(s_cur, 1)
                    take_node_major(N_LAYERS + l)
            dve.wait_ge(s_evac, FREE + 2 * N_LAYERS * GROUPS)
            dve.wait_ge(s_res, GROUPS)
            layer_norm(1)


_INS = ['x', 'src', 'dst', 'firsts', 'edge_weight', 'L0_gnn_weight', 'L0_gnn_w_ih', 'L0_gnn_w_hh', 'L0_gnn_b_ih', 'L0_gnn_b_hh',
        'L1_gnn_W0', 'L1_gnn_b0', 'L1_gnn_W1', 'L1_gnn_b1', 'L1_gnn_W2', 'L1_gnn_b2']


def kernel(**inputs):
    import numpy as _np
    import concourse.bacc as _bacc
    from concourse import mybir as _mybir
    from concourse.bass_utils import run_bass_kernel_spmd as _run

    nc = _bacc.Bacc("TRN2", target_bir_lowering=False, num_devices=1)
    inputs["firsts"] = inputs["dst"][::EB]
    arrays, args = {}, []
    for name in _INS:
        a = _np.ascontiguousarray(inputs[name])
        arrays[f"in_{name}"] = a
        args.append(nc.dram_tensor(f"in_{name}", a.shape, _mybir.dt.from_np(a.dtype), kind="ExternalInput").ap())
    args.append(nc.dram_tensor("out_0", (N_NODES, P), _mybir.dt.float32, kind="ExternalOutput").ap())
    gnn_program(nc, *args)
    r = _run(nc, [arrays], core_ids=[0])
    return r.results[0]["out_0"]
```
